# Optimizing a Trainium2 kernel written in Bass

```python
import numpy as np
import jax
import jax.numpy as jnp

def _softmax(x, axis=-1):
    return jax.nn.softmax(x, axis=axis)

def _gelu(x):
    return jax.nn.gelu(x, approximate=True)

def _silu(x):
    return jax.nn.silu(x)

def _sigmoid(x):
    return jax.nn.sigmoid(x)

def _layernorm(x, axis=-1, eps=1e-05):
    m = jnp.mean(x, axis=axis, keepdims=True)
    v = jnp.var(x, axis=axis, keepdims=True)
    return (x - m) / jnp.sqrt(v + eps)

def _scatter_add(tgt, idx, src, axis=0):
    return tgt.at[idx].add(src)

def _segment_sum(src, seg, n):
    return jax.ops.segment_sum(src, seg, n)
kernel_name = 'mk_macaron_d1_jaxref_r8_193f40'

def setup_inputs(seed: int=0):
    np.random.seed(seed)
    _w = jnp.asarray

    def _L0_attn_setup():
        import jax, jax.numpy as jnp
        import numpy as np
        NEG_INF = -1e+30

        def rotary_pos_emb(x):
            B, T, H, D = x.shape
            exponents = (jnp.arange(0, D, 2)[:D // 2] // D).astype(jnp.float32)
            freqs = 1.0 / jnp.power(jnp.float32(1000.0), exponents)
            theta = jnp.arange(T, dtype=jnp.float32)[:, None] * freqs[None, :]
            cos = jnp.cos(theta)[None, :, None, :]
            sin = jnp.sin(theta)[None, :, None, :]
            xr = x.astype(jnp.float32).reshape(B, T, H, D // 2, 2)
            x0, x1 = (xr[..., 0], xr[..., 1])
            out = jnp.stack([x0 * cos - x1 * sin, x0 * sin + x1 * cos], axis=-1)
            return out.reshape(B, T, H, D).astype(x.dtype)

        def attention_fwd(x, wq, wk, wv, wo, n_heads=32):
            B, T, C = x.shape
            hd = C // n_heads
            xq = (x @ wq.T).reshape(B, T, n_heads, hd)
            xk = (x @ wk.T).reshape(B, T, n_heads, hd)
            xv = (x @ wv.T).reshape(B, T, n_heads, hd)
            xq = rotary_pos_emb(xq)
            xk = rotary_pos_emb(xk)
            scale = hd ** (-0.5)
            scores = jnp.einsum('bqhd,bkhd->bhqk', xq, xk) * scale
            causal = jnp.tril(jnp.ones((T, T), dtype=bool))
            scores = jnp.where(causal[None, None], scores, NEG_INF)
            probs = jax.nn.softmax(scores.astype(jnp.float32), axis=-1).astype(xq.dtype)
            out = jnp.einsum('bhqk,bkhd->bqhd', probs, xv).reshape(B, T, C)
            return out @ wo.T
        key = jax.random.key(seed)
        ks = jax.random.split(key, 5)
        B, T, C = (2, 256, 512)
        s = 0.02
        return {'x': jax.random.normal(ks[0], (B, T, C), jnp.float32), 'wq': jax.random.normal(ks[1], (C, C), jnp.float32) * s, 'wk': jax.random.normal(ks[2], (C, C), jnp.float32) * s, 'wv': jax.random.normal(ks[3], (C, C), jnp.float32) * s, 'wo': jax.random.normal(ks[4], (C, C), jnp.float32) * s}
    _L0_attn_in = _L0_attn_setup()

    def _L0_ffn_setup():
        import jax, jax.numpy as jnp
        import numpy as np
        GROUP = 64

        def dequant_q40(w, s, out_features, in_features):
            msb = w >> 4
            lsb = (w & 15 ^ 8) - 8
            g = jnp.concatenate([msb, lsb], axis=1).reshape(-1, GROUP)
            deq = g.astype(s.dtype) * s[:, None]
            return deq.reshape(out_features, in_features)
        key = jax.random.key(seed)
        ks = jax.random.split(key, 7)
        dim, hidden = (512, 1376)
        B, S = (2, 256)

        def packed(k, din, dout):
            return jax.random.randint(k, (din * dout // GROUP // 2, GROUP), -128, 128, dtype=jnp.int32)

        def scales(k, din, dout):
            return (jax.random.uniform(k, (din * dout // GROUP,), dtype=jnp.float32) + 0.5) * 0.01
        x = jax.random.normal(ks[0], (B, S, dim), dtype=jnp.float32)
        w1 = packed(ks[1], dim, hidden)
        s1 = scales(ks[2], dim, hidden)
        w2 = packed(ks[3], hidden, dim)
        s2 = scales(ks[4], hidden, dim)
        w3 = packed(ks[5], dim, hidden)
        s3 = scales(ks[6], dim, hidden)
        return {'x': x, 'w1': w1, 's1': s1, 'w2': w2, 's2': s2, 'w3': w3, 's3': s3}
    _L0_ffn_in = _L0_ffn_setup()
    _d = {'L0_attn_x': _L0_attn_in['x'], 'L0_attn_wq': _L0_attn_in['wq'], 'L0_attn_wk': _L0_attn_in['wk'], 'L0_attn_wv': _L0_attn_in['wv'], 'L0_attn_wo': _L0_attn_in['wo'], 'L0_ffn_w1': _L0_ffn_in['w1'], 'L0_ffn_s1': _L0_ffn_in['s1'], 'L0_ffn_w2': _L0_ffn_in['w2'], 'L0_ffn_s2': _L0_ffn_in['s2'], 'L0_ffn_w3': _L0_ffn_in['w3'], 'L0_ffn_s3': _L0_ffn_in['s3']}
    _x0 = _d['L0_attn_x']
    _d['L0_attn_x'] = jax.random.normal(jax.random.fold_in(jax.random.key(seed), 1), (2, 1024, 512), dtype=_x0.dtype)
    del _x0
    return _d

def reference(L0_attn_x, L0_attn_wq, L0_attn_wk, L0_attn_wv, L0_attn_wo, L0_ffn_w1, L0_ffn_s1, L0_ffn_w2, L0_ffn_s2, L0_ffn_w3, L0_ffn_s3):

    def _L0_attn_ref(x, wq, wk, wv, wo):
        import jax, jax.numpy as jnp
        import numpy as np
        NEG_INF = -1e+30

        def rotary_pos_emb(x):
            B, T, H, D = x.shape
            exponents = (jnp.arange(0, D, 2)[:D // 2] // D).astype(jnp.float32)
            freqs = 1.0 / jnp.power(jnp.float32(1000.0), exponents)
            theta = jnp.arange(T, dtype=jnp.float32)[:, None] * freqs[None, :]
            cos = jnp.cos(theta)[None, :, None, :]
            sin = jnp.sin(theta)[None, :, None, :]
            xr = x.astype(jnp.float32).reshape(B, T, H, D // 2, 2)
            x0, x1 = (xr[..., 0], xr[..., 1])
            out = jnp.stack([x0 * cos - x1 * sin, x0 * sin + x1 * cos], axis=-1)
            return out.reshape(B, T, H, D).astype(x.dtype)

        def attention_fwd(x, wq, wk, wv, wo, n_heads=32):
            B, T, C = x.shape
            hd = C // n_heads
            xq = (x @ wq.T).reshape(B, T, n_heads, hd)
            xk = (x @ wk.T).reshape(B, T, n_heads, hd)
            xv = (x @ wv.T).reshape(B, T, n_heads, hd)
            xq = rotary_pos_emb(xq)
            xk = rotary_pos_emb(xk)
            scale = hd ** (-0.5)
            scores = jnp.einsum('bqhd,bkhd->bhqk', xq, xk) * scale
            causal = jnp.tril(jnp.ones((T, T), dtype=bool))
            scores = jnp.where(causal[None, None], scores, NEG_INF)
            probs = jax.nn.softmax(scores.astype(jnp.float32), axis=-1).astype(xq.dtype)
            out = jnp.einsum('bhqk,bkhd->bqhd', probs, xv).reshape(B, T, C)
            return out @ wo.T
        return attention_fwd(x, wq, wk, wv, wo)

    def _L0_ffn_ref(x, w1, s1, w2, s2, w3, s3):
        import jax, jax.numpy as jnp
        import numpy as np
        GROUP = 64

        def dequant_q40(w, s, out_features, in_features):
            msb = w >> 4
            lsb = (w & 15 ^ 8) - 8
            g = jnp.concatenate([msb, lsb], axis=1).reshape(-1, GROUP)
            deq = g.astype(s.dtype) * s[:, None]
            return deq.reshape(out_features, in_features)
        dim = x.shape[-1]
        hidden = w1.shape[0] * w1.shape[1] * 2 // dim
        W1 = dequant_q40(w1, s1, hidden, dim)
        W3 = dequant_q40(w3, s3, hidden, dim)
        W2 = dequant_q40(w2, s2, dim, hidden)
        a = jnp.einsum('bsd,hd->bsh', x, W1)
        b = jnp.einsum('bsd,hd->bsh', x, W3)
        h = jax.nn.silu(a) * b
        return jnp.einsum('bsh,dh->bsd', h, W2)
    x = L0_attn_x
    x = x + 0.5 * _L0_ffn_ref(_layernorm(x, axis=-1), L0_ffn_w1, L0_ffn_s1, L0_ffn_w2, L0_ffn_s2, L0_ffn_w3, L0_ffn_s3)
    x = x + _L0_attn_ref(_layernorm(x, axis=-1), L0_attn_wq, L0_attn_wk, L0_attn_wv, L0_attn_wo)
    x = x + 0.5 * _L0_ffn_ref(_layernorm(x, axis=-1), L0_ffn_w1, L0_ffn_s1, L0_ffn_w2, L0_ffn_s2, L0_ffn_w3, L0_ffn_s3)
    return x

_drawn_inputs = setup_inputs


def setup_inputs(seed=0):
    import zlib

    import numpy as np

    out = dict(_drawn_inputs(seed))
    spreads = {}
    factors = {'L0_attn_wq': 8.0, 'L0_attn_wk': 8.0, 'L0_attn_wv': 3.833, 'L0_attn_wo': 3.804}
    for name, (base, spread) in spreads.items():
        noise = np.random.default_rng([zlib.crc32(name.encode()), seed]).standard_normal(out[name].shape)
        drawn = base * np.exp(spread * noise) if base else spread * noise
        out[name] = jnp.asarray(drawn.astype(out[name].dtype))
    for name, factor in factors.items():
        out[name] = (out[name] * factor).astype(out[name].dtype)
    return out
```

```python
from contextlib import ExitStack

import numpy as np

import concourse.bass as bass
from concourse import mybir

F32 = mybir.dt.float32
F32R = mybir.dt.float32r
BF16 = mybir.dt.bfloat16
I32 = mybir.dt.int32
ALU = mybir.AluOpType
ACT = mybir.ActivationFunctionType
AX = mybir.AxisListType

P = 128
B, T, C = 2, 1024, 512
TOK = B * T
H, D = 32, 16
HID = 1376
GROUP = 64
KC = C // P
HT = -(-HID // P)
HLAST = HID - (HT - 1) * P
TILES = TOK // P
CHUNK = 512
CT = CHUNK // P
NCH = TOK // CHUNK
EPS = 1e-5
SCALE = D ** -0.5
NEG = -1e30
QUADS = B * H // 4
QT = T // P
ONES = D + 1
PARTS = 3


def hidden_rows(ht):
    return P if ht < HT - 1 else HLAST


def wait_alone(eng, sem, value, sure, least):
    value = eng.to_reg(value)
    eng.wait_ge(sure, least)
    eng.wait_ge(sem, value)


def parts_of_product(high_a, low_a, high_b, low_b):
    return ((high_a, high_b), (high_a, low_b), (low_a, high_b))


def weights_phase(nc, d, k):
    packs = [
        ("w1", k.w1h, k.w1l),
        ("w3", k.w3h, k.w3l),
        ("w2", k.w2h, k.w2l),
    ]
    RPP = 4 * HT
    R2 = HID * C // (2 * GROUP) // P
    BANKS = 6
    with ExitStack() as ctx:
        sb = lambda n, s, t: ctx.enter_context(nc.sbuf_tensor(n, s, t))
        sem = lambda n: ctx.enter_context(nc.semaphore(n))
        packed = [sb(f"packed{i}", [P, RPP, GROUP], I32) for i in range(2)]
        scales = [sb(f"scales{i}", [P, RPP, 2], F32) for i in range(3)]
        deq = [sb(f"deq{i}", [P, RPP, 2, GROUP], F32) for i in range(2)]
        xs = [sb(f"xs{i}", [P, C], F32) for i in range(2)]
        turned = [ctx.enter_context(nc.psum_tensor(f"wt{i}", [P, 4, P], F32)) for i in range(BANKS)]

        packed_in = [sem(f"w_packed_in{i}") for i in range(3)]
        unpacked = sem("w_unpacked")
        scaled = sem("w_scaled")
        step = sem("w_step")
        cleared = sem("w_cleared")
        turned_ok = sem("w_turned")
        high_ok = sem("w_high")
        low_ok = sem("w_low")
        ident_ok = sem("w_ident")
        ident_z = sem("w_ident_zero")
        x_in = [sem(f"w_x_in{i}") for i in range(2)]
        x_seen = sem("w_x_seen")
        var_ok = sem("w_var")
        std_ok = sem("w_std")
        rope_in = sem("w_rope_in")

        def source(w, g):
            flat = deq[w % 2][:, :, :, :].rearrange("p r s c -> p (r s c)")
            if w < 2:
                n = hidden_rows(g)
                return [flat[0:n, g * C + c * P:g * C + (c + 1) * P] for c in range(KC)], P, n
            n = hidden_rows(g)
            return [flat[:, b * HID + g * P:b * HID + g * P + n] for b in range(4)], n, P

        def target(w, g, part):
            if w < 2:
                return part[:, :, g * P:g * P + hidden_rows(g)]
            return part[0:hidden_rows(g), g, :].rearrange("h (p b) -> h b p", b=4)

        def bank(w, g):
            _, rows, cols = source(w, g)
            return turned[(w * HT + g) % BANKS][0:rows, :, 0:cols]

        with nc.Block() as block:
            @block.sync
            def _(sp):
                for w, (name, _, _) in enumerate(packs):
                    src, sc = d[name], d["s" + name[1]]
                    if w >= 2:
                        sp.wait_ge(unpacked, w - 1)
                    if w < 2:
                        full = (HT - 1) * P
                        sp.wait_ge(cleared, 4)
                        sp.dma_start(packed[w][:, 0:4 * (HT - 1), :].rearrange("p (t r) c -> p t (r c)", r=4),
                                     src[0:4 * full, :].rearrange("(t p r) c -> p t (r c)", p=P, r=4)
                                     ).then_inc(packed_in[w], 16)
                        sp.dma_start(packed[w][0:HLAST, 4 * (HT - 1):RPP, :].rearrange("p r c -> p (r c)"),
                                     src[4 * full:4 * HID, :].rearrange("(p r) c -> p (r c)", r=4)
                                     ).then_inc(packed_in[w], 16)
                        sp.dma_start(scales[w][:, 0:4 * (HT - 1), :].rearrange("p (t r) s -> p t (r s)", r=4),
                                     sc[0:8 * full].rearrange("(t p g) -> p t g", p=P, g=8)
                                     ).then_inc(packed_in[w], 16)
                        sp.dma_start(scales[w][0:HLAST, 4 * (HT - 1):RPP, :].rearrange("p r s -> p (r s)"),
                                     sc[8 * full:8 * HID].rearrange("(p g) -> p g", g=8)
                                     ).then_inc(packed_in[w], 16)
                    else:
                        sp.dma_start(packed[w % 2][:, 0:R2, :].rearrange("p r c -> p (r c)"),
                                     src.rearrange("(p r) c -> p (r c)", p=P)).then_inc(packed_in[w], 16)
                        sp.dma_start(scales[w][:, 0:R2, :].rearrange("p r s -> p (r s)"),
                                     sc.rearrange("(p g) -> p g", p=P)).then_inc(packed_in[w], 16)

            @block.gpsimd
            def _(pool):
                for w in range(2):
                    pool.memset(packed[w][:, 4 * (HT - 1):RPP, :], 0).then_inc(cleared, 1)
                    pool.memset(scales[w][:, 4 * (HT - 1):RPP, :], 0.0).then_inc(cleared, 1)
                pool.memset(k.ident[:, :], 0.0).then_inc(ident_z, 1)
                pool.wait_ge(ident_z, 1)
                pool.affine_select(out=k.ident[:, :], in_=k.ident[:, :], compare_op=ALU.not_equal, fill=1.0,
                                   base=0, pattern=[[-1, P]], channel_multiplier=1).then_inc(ident_ok, 1)
                pool.dma_start(k.rope[:, :, :], d["rope"]).then_inc(rope_in, 16)
                for t in range(TILES):
                    if t >= 2:
                        pool.wait_ge(x_seen, t - 1)
                    pool.dma_start(xs[t % 2][:, :], d["x"][t * P:(t + 1) * P, :]).then_inc(x_in[t % 2], 16)
                pool.wait_ge(rope_in, 16)

            @block.vector
            def _(dve):
                steps = [0]

                def unpack(w):
                    rows = RPP if w < 2 else R2
                    src, out = packed[w % 2][:, 0:rows, :], deq[w % 2][:, 0:rows, :, :]
                    bits = out.bitcast(I32)
                    dve.wait_ge(packed_in[w], 64 if w < 2 else 32)
                    if w >= 2:
                        dve.wait_ge(low_ok, (w - 1) * HT)
                    nc.vector.tensor_scalar(bits[:, :, 0, :], src, 4, None, ALU.arith_shift_right)
                    nc.vector.tensor_scalar(bits[:, :, 1, :], src, 15, 8, ALU.bitwise_and,
                                            ALU.bitwise_xor).then_inc(unpacked, 1)
                    dve.wait_ge(unpacked, w + 1)
                    for s in range(2):
                        by = scales[w][:, 0:rows, s:s + 1].broadcast_to([P, rows, GROUP])
                        nc.vector.scalar_tensor_tensor(out=out[:, :, s, :], in0=bits[:, :, s, :],
                                                       scalar=-8.0 * s, in1=by, op0=ALU.add,
                                                       op1=ALU.mult).then_inc(scaled, 1)

                def low_parts(w):
                    for g in range(HT):
                        dve.wait_ge(high_ok, w * HT + g + 1)
                        nc.vector.tensor_tensor(target(w, g, packs[w][2]), bank(w, g),
                                                target(w, g, packs[w][1]).bitcast(F32),
                                                ALU.subtract).then_inc(low_ok, 1)

                unpack(0)
                unpack(1)
                low_parts(0)
                unpack(2)
                low_parts(1)
                low_parts(2)
                for t in range(TILES):
                    dve.wait_ge(x_in[t % 2], 16 * (t // 2 + 1))
                    nc.vector.bn_stats(k.stats[:, t, :], xs[t % 2][:, :]).then_inc(x_seen, 1)
                dve.wait_ge(x_seen, TILES)
                layernorm_factors(nc, dve, k, step, var_ok, std_ok)

            @block.scalar
            def _(act):
                for w in range(3):
                    for g in range(HT):
                        act.wait_ge(turned_ok, w * HT + g + 1)
                        nc.scalar.activation(target(w, g, packs[w][1]), bank(w, g), ACT.Copy).then_inc(high_ok, 1)
                act.wait_ge(var_ok, 1)
                nc.scalar.activation(k.std[:, :], k.var[:, :], ACT.Sqrt).then_inc(std_ok, 1)

            @block.tensor
            def _(pe):
                pe.wait_ge(ident_ok, 1)
                for w in range(3):
                    pe.wait_ge(scaled, 2 * (w + 1))
                    for g in range(HT):
                        n = w * HT + g
                        if n >= BANKS:
                            pe.wait_ge(low_ok, n - BANKS + 1)
                        blocks, rows, cols = source(w, g)
                        for b, blk in enumerate(blocks):
                            at = turned[n % BANKS][0:rows, b, 0:cols]
                            last = nc.tensor.transpose(at, blk, k.ident[0:blk.shape[0], 0:blk.shape[0]])
                        last.then_inc(turned_ok, 1)


def layernorm_factors(nc, dve, k, step, var_ok, std_ok):
    for t in range(TILES):
        last = nc.vector.bn_aggr(k.moments[:, t, :], k.stats[:, t, :])
    last.then_inc(step, 1)
    dve.wait_ge(step, 1)
    nc.vector.tensor_scalar(k.var[:, :], k.moments[:, :, 1], EPS, None, ALU.add).then_inc(var_ok, 1)
    nc.vector.tensor_copy(k.mean[:, :], k.moments[:, :, 0])
    dve.wait_ge(std_ok, 1)
    nc.vector.reciprocal(k.rstd[:, :], k.std[:, :]).then_inc(step, 1)
    dve.wait_ge(step, 2)


def ffn_phase(nc, k, src, dst, tag, stats):
    with ExitStack() as ctx:
        sb = lambda n, s, t: ctx.enter_context(nc.sbuf_tensor(tag + n, s, t))
        ps = lambda n, s: ctx.enter_context(nc.psum_tensor(tag + n, s, F32))
        sem = lambda n: ctx.enter_context(nc.semaphore(tag + n))
        xnh = sb("xnh", [P, KC, CHUNK], F32R)
        xnl = sb("xnl", [P, KC, CHUNK], F32R)
        gh = sb("gh", [P, HT, CHUNK], F32R)
        gl = sb("gl", [P, HT, CHUNK], F32R)
        xr = [sb(f"xr{i}", [P, C], F32) for i in range(2)]
        sa = [sb(f"sa{i}", [P, CHUNK], F32) for i in range(2)]
        g32 = [sb(f"g{i}", [P, CHUNK], F32) for i in range(2)]
        res = [sb(f"res{i}", [P, C], F32) for i in range(2)]
        pa = [ps(f"pa{i}", [P, CHUNK]) for i in range(2)]
        pb = [ps(f"pb{i}", [P, CHUNK]) for i in range(2)]
        pt = [ps(f"pt{i}", [P, KC, P]) for i in range(2)]
        py = [ps(f"py{i}", [P, C]) for i in range(2)]

        x_in = [sem(f"x_in{i}") for i in range(2)]
        xn_ok = sem("xn_ok")
        xt_ok = sem("xt_ok")
        xh_ok = sem("xh_ok")
        xl_ok = sem("xl_ok")
        ab_ok = sem("ab_ok")
        sa_ok = sem("sa_ok")
        g_ok = sem("g_ok")
        gh_ok = sem("gh_ok")
        gl_ok = sem("gl_ok")
        y_ok = sem("y_ok")
        r_in = [sem(f"r_in{i}") for i in range(2)]
        out_ok = sem("out_ok")
        stat_ok = sem("stat_ok")
        stored = [sem(f"stored{i}") for i in range(2)]
        step, var_ok, std_ok = sem("step"), sem("var_ok"), sem("std_ok")

        def rows(n):
            return src[bass.ds((n & (TILES - 1)) * P, P), :] if not isinstance(n, int) else src[n * P:(n + 1) * P, :]

        with nc.Block() as block:
            @block.sync
            def _(sp):
                for t in range(2):
                    sp.dma_start(xr[t][:, :], rows(t)).then_inc(x_in[t], 16)
                for t in range(2, CT):
                    sp.wait_ge(xt_ok, t - 1)
                    sp.dma_start(xr[t % 2][:, :], rows(t)).then_inc(x_in[t % 2], 16)
                for t in range(2):
                    sp.dma_start(res[t][:, :], rows(t)).then_inc(r_in[t], 16)

                def load_next(c, t):
                    wait_alone(sp, xt_ok, c * CT + CT + t - 1, x_in[0], 16)
                    sp.dma_start(xr[t % 2][:, :], rows(c * CT + CT + t)).then_inc(x_in[t % 2], 16)

                def store(c, t):
                    wait_alone(sp, stat_ok, c * CT + t + 1, x_in[0], 16)
                    sp.dma_start(dst[bass.ds((c * CT + t) * P, P), :], res[t % 2][:, :]).then_inc(stored[t % 2], 16)

                def load_residual(c, t):
                    wait_alone(sp, stored[t % 2], c * 32 + (t // 2 + 1) * 16, x_in[0], 16)
                    sp.dma_start(res[t % 2][:, :], rows(c * CT + t + 2)).then_inc(r_in[t % 2], 16)

                with sp.Fori(0, NCH) as c:
                    load_next(c, 0)
                    load_next(c, 1)
                    load_next(c, 2)
                    store(c, 0)
                    load_residual(c, 0)
                    load_next(c, 3)
                    for t in range(1, CT):
                        store(c, t)
                        load_residual(c, t)
                for i in range(2):
                    sp.wait_ge(stored[i], 16 * TILES // 2)
                    sp.wait_ge(r_in[i], 16 * (TILES // 2 + 1))
                    sp.wait_ge(x_in[i], 16 * (TILES + CT) // 2)

            @block.vector
            def _(dve):
                def normalise(n, t, k_in):
                    dve.wait_ge(x_in[t % 2], k_in)
                    at = (n & (TILES - 1)) if not isinstance(n, int) else n
                    nc.vector.tensor_scalar(xr[t % 2][:, :], xr[t % 2][:, :], k.mean[:, bass.ds(at, 1)],
                                            k.rstd[:, bass.ds(at, 1)], ALU.subtract, ALU.mult).then_inc(xn_ok, 1)

                def low_part(n, t):
                    dve.wait_ge(xh_ok, n + 1)
                    at = slice(t * P, (t + 1) * P)
                    nc.vector.tensor_tensor(xnl[:, :, at], pt[t % 2][:, :, :], xnh[:, :, at].bitcast(F32),
                                            ALU.subtract).then_inc(xl_ok, 1)

                for t in range(CT):
                    normalise(t, t, 16 * (t // 2 + 1))
                    low_part(t, t)

                with dve.Fori(0, NCH) as c:
                    for ht in range(HT):
                        n = hidden_rows(ht)
                        dve.wait_ge(sa_ok, c * HT + ht + 1)
                        if ht >= 2:
                            dve.wait_ge(gl_ok, c * HT + ht - 1)
                        nc.vector.tensor_tensor(g32[ht % 2][0:n, :], sa[ht % 2][0:n, :], pb[ht % 2][0:n, :],
                                                ALU.mult).then_inc(g_ok, 1)
                        if ht in (4, 6):
                            t = (ht - 4) // 2
                            normalise(c * CT + CT + t, t, c * 32 + 48)
                    for t in range(CT):
                        low_part(c * CT + CT + t, t)
                        if t < 2:
                            normalise(c * CT + CT + t + 2, t, c * 32 + 64)
                        dve.wait_ge(y_ok, c * CT + t + 1)
                        dve.wait_ge(r_in[t % 2], c * 32 + (t // 2 + 1) * 16)
                        nc.vector.scalar_tensor_tensor(out=res[t % 2][:, :], in0=py[t % 2][:, :], scalar=0.5,
                                                       in1=res[t % 2][:, :], op0=ALU.mult,
                                                       op1=ALU.add).then_inc(out_ok, 1)
                        dve.wait_ge(out_ok, c * CT + t + 1)
                        if stats:
                            nc.vector.bn_stats(k.stats[:, bass.ds(c * CT + t, 1), :].rearrange("p a s -> p (a s)"),
                                               res[t % 2][:, :]).then_inc(stat_ok, 1)
                        else:
                            dve.sem_inc(stat_ok, 1)
                if stats:
                    dve.wait_ge(stat_ok, TILES)
                    layernorm_factors(nc, dve, k, step, var_ok, std_ok)

            @block.scalar
            def _(act):
                def high_part(n, t):
                    act.wait_ge(xt_ok, n + 1)
                    if isinstance(n, int) and n >= 2:
                        act.wait_ge(xl_ok, n - 1)
                    nc.scalar.activation(xnh[:, :, t * P:(t + 1) * P], pt[t % 2][:, :, :], ACT.Copy).then_inc(xh_ok, 1)

                for t in range(CT):
                    high_part(t, t)
                with act.Fori(0, NCH) as c:
                    for ht in range(HT):
                        n = hidden_rows(ht)
                        act.wait_ge(ab_ok, c * HT + ht + 1)
                        if ht >= 2:
                            act.wait_ge(g_ok, c * HT + ht - 1)
                        nc.scalar.activation(sa[ht % 2][0:n, :], pa[ht % 2][0:n, :], ACT.Silu).then_inc(sa_ok, 1)
                        act.wait_ge(g_ok, c * HT + ht + 1)
                        nc.scalar.activation(gh[0:n, ht, :], g32[ht % 2][0:n, :], ACT.Copy).then_inc(gh_ok, 1)
                    for t in range(CT):
                        high_part(c * CT + CT + t, t)
                if stats:
                    act.wait_ge(var_ok, 1)
                    nc.scalar.activation(k.std[:, :], k.var[:, :], ACT.Sqrt).then_inc(std_ok, 1)

            @block.gpsimd
            def _(pool):
                with pool.Fori(0, NCH) as c:
                    for ht in range(HT):
                        n = hidden_rows(ht)
                        pool.wait_ge(gh_ok, c * HT + ht + 1)
                        nc.gpsimd.tensor_tensor(gl[0:n, ht, :], g32[ht % 2][0:n, :], gh[0:n, ht, :].bitcast(F32),
                                                ALU.subtract).then_inc(gl_ok, 1)

            @block.tensor
            def _(pe):
                def turn(n, t):
                    pe.wait_ge(xn_ok, n + 1)
                    if not isinstance(n, int) or n >= 2:
                        pe.wait_ge(xl_ok, n - 1)
                    for c4 in range(KC):
                        last = nc.tensor.transpose(pt[t % 2][:, c4, :], xr[t % 2][:, c4 * P:(c4 + 1) * P],
                                                   k.ident[:, :])
                    last.then_inc(xt_ok, 1)

                def product(out, wh, wl, ht):
                    n = hidden_rows(ht)
                    pairs = [(w[:, c4, ht * P:ht * P + n], x[:, c4, :])
                             for c4 in range(KC) for w, x in parts_of_product(wh, wl, xnh, xnl)]
                    for i, (w, x) in enumerate(pairs):
                        last = nc.tensor.matmul(out, w, x, start=i == 0, stop=i == len(pairs) - 1)
                    return last

                for t in range(CT):
                    turn(t, t)
                with pe.Fori(0, NCH) as c:
                    pe.wait_ge(xl_ok, c * CT + CT)
                    for ht in range(HT):
                        n = hidden_rows(ht)
                        if ht >= 2:
                            pe.wait_ge(g_ok, c * HT + ht - 1)
                        product(pa[ht % 2][0:n, :], k.w1h, k.w1l, ht)
                        product(pb[ht % 2][0:n, :], k.w3h, k.w3l, ht).then_inc(ab_ok, 1)
                    for t in range(CT):
                        turn(c * CT + CT + t, t)
                        if t >= 2:
                            pe.wait_ge(out_ok, c * CT + t - 1)
                        for ht in range(HT):
                            n = hidden_rows(ht)
                            if t == 0:
                                pe.wait_ge(gl_ok, c * HT + ht + 1)
                            at = slice(t * P, (t + 1) * P)
                            for i, (g, w) in enumerate(parts_of_product(gh, gl, k.w2h, k.w2l)):
                                last = nc.tensor.matmul(py[t % 2][:, :], g[0:n, ht, at], w[0:n, ht, :],
                                                        start=ht == 0 and i == 0, stop=ht == HT - 1 and i == 2)
                        last.then_inc(y_ok, 1)


def turn_weights(nc, k, sources, parts, tag):
    with ExitStack() as ctx:
        nat = [ctx.enter_context(nc.sbuf_tensor(f"{tag}nat{i}", [P, KC, C], F32)) for i in range(2)]
        pt = [ctx.enter_context(nc.psum_tensor(f"{tag}pt{i}", [P, C], F32)) for i in range(4)]
        sem = lambda n: ctx.enter_context(nc.semaphore(tag + n))
        w_in, turned, high, low = [sem(f"w_in{i}") for i in range(2)], sem("turned"), sem("high"), sem("low")
        n_w = len(sources)
        with nc.Block() as block:
            @block.sync
            def _(sp):
                for w in range(n_w):
                    if w >= 2:
                        sp.wait_ge(turned, KC * (w - 1))
                    sp.dma_start(nat[w % 2][:, :, :], sources[w].rearrange("(o p) i -> p o i", p=P)
                                 ).then_inc(w_in[w % 2], 16)

            @block.tensor
            def _(pe):
                for w in range(n_w):
                    pe.wait_ge(w_in[w % 2], 16 * (w // 2 + 1))
                    for c4 in range(KC):
                        n = w * KC + c4
                        if n >= 4:
                            pe.wait_ge(low, n - 3)
                        for o in range(KC):
                            last = nc.tensor.transpose(pt[n % 4][:, o * P:(o + 1) * P],
                                                       nat[w % 2][:, o, c4 * P:(c4 + 1) * P], k.ident[:, :])
                        last.then_inc(turned, 1)

            @block.scalar
            def _(act):
                for n in range(n_w * KC):
                    act.wait_ge(turned, n + 1)
                    nc.scalar.activation(parts[n // KC][0][:, n % KC, :], pt[n % 4][:, :], ACT.Copy).then_inc(high, 1)

            @block.vector
            def _(dve):
                for n in range(n_w * KC):
                    dve.wait_ge(high, n + 1)
                    nc.vector.tensor_tensor(parts[n // KC][1][:, n % KC, :], pt[n % 4][:, :],
                                            parts[n // KC][0][:, n % KC, :].bitcast(F32),
                                            ALU.subtract).then_inc(low, 1)


def qkv_phase(nc, d, k, src):
    with ExitStack() as ctx:
        sb = lambda n, s, t: ctx.enter_context(nc.sbuf_tensor(n, s, t))
        ps = lambda n, s: ctx.enter_context(nc.psum_tensor(n, s, F32))
        sem = lambda n: ctx.enter_context(nc.semaphore("q_" + n))
        parts = [(sb(f"{w}h", [P, KC, C], F32R), sb(f"{w}l", [P, KC, C], F32R)) for w in ("wq", "wk", "wv")]
        turn_weights(nc, k, [d["wq"], d["wk"], d["wv"]], parts, "tq_")

        xr = [sb(f"qxr{i}", [P, C], F32) for i in range(2)]
        xh = [sb(f"qxh{i}", [P, KC, P], F32R) for i in range(2)]
        xl = [sb(f"qxl{i}", [P, KC, P], F32R) for i in range(2)]
        turn = [sb(f"turn{i}", [P, 3], F32) for i in range(2)]
        by_cos = sb("by_cos", [P, C], F32)
        roped = [sb(f"roped{i}", [P, C], F32) for i in range(2)]
        th = [sb(f"th{i}", [P, KC, P], F32R) for i in range(2)]
        tl = [sb(f"tl{i}", [P, KC, P], F32R) for i in range(2)]
        va = sb("va", [P, H, ONES], F32)
        pt = ps("q_pt", [P, KC, P])
        pj = [ps(f"q_pj{i}", [P, C]) for i in range(3)]
        pr = [ps(f"q_pr{i}", [P, KC, P]) for i in range(2)]

        x_in = [sem(f"x_in{i}") for i in range(2)]
        xn_ok, xt_ok, xh_ok, xl_ok = sem("xn_ok"), sem("xt_ok"), sem("xh_ok"), sem("xl_ok")
        pj_ok = [sem(f"pj_ok{i}") for i in range(3)]
        cos_ok = [sem(f"cos_ok{i}") for i in range(2)]
        rope_ok = [sem(f"rope_ok{i}") for i in range(2)]
        v_ok = sem("v_ok")
        rt_ok = [sem(f"rt_ok{i}") for i in range(2)]
        th_ok = [sem(f"th_ok{i}") for i in range(2)]
        tl_ok = [sem(f"tl_ok{i}") for i in range(2)]
        th_out = [sem(f"th_out{i}") for i in range(2)]
        tl_out = [sem(f"tl_out{i}") for i in range(2)]
        v_out = sem("v_out")
        ones_ok = sem("ones_ok")

        def rows(n):
            return src[bass.ds((n & (TILES - 1)) * P, P), :] if not isinstance(n, int) else src[n * P:(n + 1) * P, :]

        with nc.Block() as block:
            @block.sync
            def _(sp):
                for t in range(2):
                    sp.dma_start(xr[t][:, :], rows(t)).then_inc(x_in[t], 16)
                for b in range(B):
                    with sp.Fori(0, QT // 2) as j:
                        i = j + b * (QT // 2)
                        for s in range(2):
                            wait_alone(sp, xt_ok, 2 * i + s + 1, x_in[0], 16)
                            sp.dma_start(xr[s][:, :], rows(2 * i + s + 2)).then_inc(x_in[s], 16)
                            toks = bass.ds((2 * j + s) * P, P)
                            rowsb = slice(b * C, (b + 1) * C)
                            for m, (hi, lo) in enumerate(((k.qh, k.ql), (k.kh, k.kl))):
                                wait_alone(sp, th_ok[m], 2 * i + s + 1, x_in[0], 16)
                                sp.dma_start(hi[rowsb, toks].rearrange("(g p) q -> p g q", p=P),
                                             th[m][:, :, :].bitcast(F32)).then_inc(th_out[m], 16)
                                wait_alone(sp, tl_ok[m], 2 * i + s + 1, x_in[0], 16)
                                sp.dma_start(lo[rowsb, toks].rearrange("(g p) q -> p g q", p=P),
                                             tl[m][:, :, :].bitcast(F32)).then_inc(tl_out[m], 16)
                            wait_alone(sp, v_ok, 2 * i + s + 1, x_in[0], 16)
                            sp.dma_start(k.v[b * (H // 4):(b + 1) * (H // 4), toks, :].rearrange("a q c -> q a c"),
                                         va[:, :, :].rearrange("p (a h) c -> p a (h c)", h=4)).then_inc(v_out, 16)
                for m in range(2):
                    sp.wait_ge(th_out[m], 16 * TILES)
                    sp.wait_ge(tl_out[m], 16 * TILES)
                    sp.wait_ge(x_in[m], 16 * (TILES // 2 + 1))
                sp.wait_ge(v_out, 16 * TILES)

            @block.gpsimd
            def _(pool):
                pool.memset(va[:, :, :], 1.0).then_inc(ones_ok, 1)

            @block.vector
            def _(dve):
                def normalise(n, s, count):
                    dve.wait_ge(x_in[s], count)
                    at = (n & (TILES - 1)) if not isinstance(n, int) else n
                    nc.vector.tensor_scalar(xr[s][:, :], xr[s][:, :], k.mean[:, bass.ds(at, 1)],
                                            k.rstd[:, bass.ds(at, 1)], ALU.subtract, ALU.mult).then_inc(xn_ok, 1)

                def low_x(n, s):
                    dve.wait_ge(xh_ok, n + 1)
                    nc.vector.tensor_tensor(xl[s][:, :, :], pt[:, :, :], xh[s][:, :, :].bitcast(F32),
                                            ALU.subtract).then_inc(xl_ok, 1)

                def angles(n, s):
                    at = (n & (QT - 1)) if not isinstance(n, int) else n
                    nc.vector.tensor_copy(turn[s][:, :].unsqueeze(2), k.rope[:, :, bass.ds(at, 1)])

                def rotate(n, s, m):
                    dve.wait_ge(cos_ok[m], n + 1)
                    pairs = lambda a: a[:, :].rearrange("p (h two) -> p h two", two=2)
                    x, c, o = pairs(pj[m]), pairs(by_cos), pairs(roped[m])
                    nc.vector.scalar_tensor_tensor(out=o[:, :, 0], in0=x[:, :, 1], scalar=turn[s][:, 2:3],
                                                   in1=c[:, :, 0], op0=ALU.mult, op1=ALU.add)
                    nc.vector.scalar_tensor_tensor(out=o[:, :, 1], in0=x[:, :, 0], scalar=turn[s][:, 1:2],
                                                   in1=c[:, :, 1], op0=ALU.mult, op1=ALU.add).then_inc(rope_ok[m], 1)

                def low_t(n, m, first):
                    dve.wait_ge(th_ok[m], n + 1)
                    if not first:
                        dve.wait_ge(tl_out[m], 16 * n)
                    nc.vector.tensor_tensor(tl[m][:, :, :], pr[m][:, :, :], th[m][:, :, :].bitcast(F32),
                                            ALU.subtract).then_inc(tl_ok[m], 1)

                def tile(n, s, count, first=False):
                    rotate(n, s, 0)
                    low_x(n + 1, 1 - s)
                    normalise(n + 2, s, count)
                    rotate(n, s, 1)
                    dve.wait_ge(rope_ok[1], n + 1)
                    angles(n + 2, s)
                    low_t(n, 0, first)
                    low_t(n, 1, first)

                angles(0, 0)
                angles(1, 1)
                normalise(0, 0, 16)
                normalise(1, 1, 16)
                low_x(0, 0)
                tile(0, 0, 32, True)
                tile(1, 1, 32)
                with dve.Fori(1, TILES // 2) as i:
                    for s in range(2):
                        tile(2 * i + s, s, i * 16 + 32)

            @block.scalar
            def _(act):
                def high_x(n, s):
                    act.wait_ge(xt_ok, n + 1)
                    nc.scalar.activation(xh[s][:, :, :], pt[:, :, :], ACT.Copy).then_inc(xh_ok, 1)

                def cos_part(n, s, m, first):
                    act.wait_ge(pj_ok[m], n + 1)
                    if m == 1:
                        act.wait_ge(rope_ok[0], n + 1)
                    elif not first:
                        act.wait_ge(rope_ok[1], n)
                    nc.scalar.activation(by_cos[:, :], pj[m][:, :], ACT.Copy,
                                         scale=turn[s][:, 0:1]).then_inc(cos_ok[m], 1)

                def tile(n, s, first=False):
                    cos_part(n, s, 0, first)
                    high_x(n + 1, 1 - s)
                    cos_part(n, s, 1, first)
                    act.wait_ge(pj_ok[2], n + 1)
                    if not first:
                        act.wait_ge(v_out, 16 * n)
                    nc.scalar.activation(va[:, :, 0:D], pj[2][:, :].rearrange("p (h c) -> p h c", c=D),
                                         ACT.Copy).then_inc(v_ok, 1)
                    for m in range(2):
                        act.wait_ge(rt_ok[m], n + 1)
                        if not first:
                            act.wait_ge(th_out[m], 16 * n)
                        nc.scalar.activation(th[m][:, :, :], pr[m][:, :, :], ACT.Copy).then_inc(th_ok[m], 1)

                high_x(0, 0)
                act.wait_ge(ones_ok, 1)
                tile(0, 0, True)
                tile(1, 1)
                with act.Fori(1, TILES // 2) as i:
                    for s in range(2):
                        tile(2 * i + s, s)

            @block.tensor
            def _(pe):
                def turn_x(n, s):
                    pe.wait_ge(xn_ok, n + 1)
                    for c4 in range(KC):
                        last = nc.tensor.transpose(pt[:, c4, :], xr[s][:, c4 * P:(c4 + 1) * P], k.ident[:, :])
                    last.then_inc(xt_ok, 1)

                def project(m, s):
                    pairs = [(x[:, c4, :], w[:, c4, :]) for c4 in range(KC)
                             for x, w in parts_of_product(xh[s], xl[s], *parts[m])]
                    for i, (x, w) in enumerate(pairs):
                        last = nc.tensor.matmul(pj[m][:, :], x, w, start=i == 0, stop=i == len(pairs) - 1)
                    last.then_inc(pj_ok[m], 1)

                def tile(n, s, first=False):
                    pe.wait_ge(xl_ok, n + 1)
                    if not first:
                        pe.wait_ge(rope_ok[0], n)
                    project(0, s)
                    turn_x(n + 1, 1 - s)
                    if not first:
                        pe.wait_ge(rope_ok[1], n)
                    project(1, s)
                    if not first:
                        pe.wait_ge(v_ok, n)
                    project(2, s)
                    for m in range(2):
                        pe.wait_ge(rope_ok[m], n + 1)
                        if not first:
                            pe.wait_ge(tl_ok[m], n)
                        for c4 in range(KC):
                            last = nc.tensor.transpose(pr[m][:, c4, :], roped[m][:, c4 * P:(c4 + 1) * P],
                                                       k.ident[:, :])
                        last.then_inc(rt_ok[m], 1)

                turn_x(0, 0)
                tile(0, 0, True)
                tile(1, 1)
                with pe.Fori(1, TILES // 2) as i:
                    for s in range(2):
                        tile(2 * i + s, s)


HALF = T // 2
HQ = QT // 2
MROW = PARTS * D
KROWS = MROW + 2


def score_units():
    units = []
    for i in range(QT):
        for half in range(i // HQ + 1):
            width = min(HALF, (i + 1) * P - half * HALF)
            together = 2 if 2 * width <= HALF else 1
            for r in range(2):
                for a in range(0, 2, together):
                    units.append((i, half, [2 * (a + x) + r for x in range(together)], width))
    first = sum(1 for u in units if u[0] < HQ)
    units.insert(first + 3, (0,))
    units.append((1,))
    return units


def attention_steps():
    return [(half, j, max(half * HALF, j * P)) for half in range(2) for j in range(HQ * (half + 1))]


def attention_phase(nc, k):
    UNITS, STEPS = score_units(), attention_steps()
    NU, NS = len(UNITS), len(STEPS)
    A_UNITS = sum(1 for u in UNITS if len(u) > 1 and u[0] < HQ)
    RING = 3
    assert NS % RING == 0
    per = [(NU - 1) * (s + 1) // (NS - 1) for s in range(NS - 1)] + [NU]
    with ExitStack() as ctx:
        sb = lambda n, s, t: ctx.enter_context(nc.sbuf_tensor("a_" + n, s, t))
        ps = lambda n, s: ctx.enter_context(nc.psum_tensor("a_" + n, s, F32))
        sem = lambda n: ctx.enter_context(nc.semaphore("a_" + n))
        qs = [sb(f"qs{i}", [P, 2, 2, HALF], F32R) for i in range(2)]
        ks = [sb(f"ks{i}", [P, 2, 2, HALF], F32R) for i in range(2)]
        vq = [sb(f"vq{i}", [P, QT, 4, ONES], F32) for i in range(2)]
        pr = [sb(f"probs{i}", [P, 4, HALF], F32) for i in range(RING)]
        osb = [sb(f"osb{i}", [P, HALF], F32) for i in range(2)]
        mx = [sb(f"rowmax{i}", [P, P], F32) for i in range(2)]
        by_half = [sb(f"max_half{i}", [P, 4 * HQ], F32) for i in range(2)]
        mh = [sb(f"mh{i}", [4 * HQ, P], F32R) for i in range(2)]
        ml = [sb(f"ml{i}", [4 * HQ, P], F32R) for i in range(2)]
        mask = sb("mask", [P, P], BF16)
        mask_t = sb("mask_t", [P, P], BF16)
        identb = sb("identb", [P, P], BF16)
        psc = [ps(f"psc{i}", [P, HALF]) for i in range(2)]
        pst = [ps(f"pst{i}", [P, 2, HALF]) for i in range(2)]
        po = [ps(f"po{i}", [P, HALF]) for i in range(2)]

        const_z, const_ok, clear_ok = sem("const_z"), sem("const_ok"), sem("clear_ok")
        qa_in = [sem(f"qa_in{i}") for i in range(2)]
        qb_in = [sem(f"qb_in{i}") for i in range(2)]
        v_in = [sem(f"v_in{i}") for i in range(2)]
        sc_ok = sem("sc_ok")
        mx_ok = sem("mx_ok")
        mxb_ok = sem("mxb_ok")
        mstep = sem("mstep")
        m_in = [sem(f"m_in{i}") for i in range(2)]
        st_ok = sem("st_ok")
        ex_ok = sem("ex_ok")
        pv_ok = sem("pv_ok")
        o_ok = [sem(f"o_ok{i}") for i in range(2)]
        o_out = [sem(f"o_out{i}") for i in range(2)]

        LOADS = 6
        MLOADS = 4

        with nc.Block() as block:
            @block.sync
            def _(sp):
                def load(it, s, half, sems):
                    at = slice(half * HALF, (half + 1) * HALF)
                    q = (2 * it + s) & (QUADS - 1) if not isinstance(it, int) else 2 * it + s
                    for stack, scratches in ((qs[s], (k.qh, k.qh, k.ql)), (ks[s], (k.kh, k.kl, k.kh))):
                        for part, scratch in enumerate(scratches):
                            src = scratch[bass.ds(q * (4 * D), 4 * D), at].rearrange("(a r d) t -> r d a t", a=2, r=2)
                            for r in range(2):
                                row = 64 * r + part * D
                                sp.dma_start(stack[row:row + D, half, :, :].bitcast(F32), src[r]).then_inc(sems[s], 16)

                def load_v(it, s):
                    q = (2 * it + s) & (QUADS - 1) if not isinstance(it, int) else 2 * it + s
                    sp.dma_start(vq[s][:, :, :, :].rearrange("p j h c -> p j (h c)"),
                                 k.v[bass.ds(q, 1), :, :].rearrange("o (j p) c -> p (o j) c", p=P)
                                 ).then_inc(v_in[s], 16)

                def put_max(q, s, half):
                    sp.wait_ge(mx_ok, q * NU + UNITS.index((half,)) + 1)
                    for r in range(2):
                        for x, m in enumerate((mh[half], ml[half])):
                            row = 64 * r + MROW + x
                            sp.dma_start(qs[s][row:row + 1, half, :, :].rearrange("o a t -> o (a t)").bitcast(F32),
                                         m[2 * HQ * r:2 * HQ * (r + 1), :].bitcast(F32)).then_inc(m_in[half], 16)

                sp.wait_ge(clear_ok, 4)
                for s in range(2):
                    load(0, s, 0, qa_in)
                    load(0, s, 1, qb_in)
                    load_v(0, s)
                put_max(0, 0, 0)
                put_max(0, 0, 1)
                with sp.Fori(0, QUADS // 2) as it:
                    for s in range(2):
                        q = 2 * it + s
                        put_max(q + 1, 1 - s, 0)
                        wait_alone(sp, pv_ok, q * NS + 2 * HQ, v_in[0], 16)
                        load(it + 1, s, 0, qa_in)
                        for half in range(2):
                            wait_alone(sp, o_ok[half], q + 2, v_in[0], 16)
                            sp.dma_start(k.o[bass.ds(q * P, P), half * HALF:(half + 1) * HALF],
                                         osb[half][:, :]).then_inc(o_out[half], 16)
                        load(it + 1, s, 1, qb_in)
                        load_v(it + 1, s)
                        put_max(q + 1, 1 - s, 1)
                for i in range(2):
                    sp.wait_ge(o_out[i], 16 * (QUADS + 1))
                    sp.wait_ge(m_in[i], 16 * MLOADS * (QUADS + 1))
                    sp.wait_ge(qa_in[i], 32 * LOADS * (QUADS // 2 + 1))
                    sp.wait_ge(qb_in[i], 32 * LOADS * (QUADS // 2 + 1))
                    sp.wait_ge(v_in[i], 16 * (QUADS // 2 + 1))

            @block.gpsimd
            def _(pool):
                for s in range(2):
                    for r in range(2):
                        pool.memset(ks[s][64 * r + 32:64 * r + 64, :, :, :].bitcast(F32), 1.0).then_inc(clear_ok, 1)
                        pool.wait_ge(clear_ok, 2 * s + r + 1)
                pool.memset(mask[:, :], 0.0).then_inc(const_z, 1)
                pool.memset(mask_t[:, :], 0.0).then_inc(const_z, 1)
                pool.memset(identb[:, :], 0.0).then_inc(const_z, 1)
                pool.wait_ge(const_z, 3)
                pool.affine_select(out=mask[:, :], in_=mask[:, :], compare_op=ALU.is_ge, fill=NEG, base=0,
                                   pattern=[[-1, P]], channel_multiplier=1).then_inc(const_ok, 1)
                pool.affine_select(out=mask_t[:, :], in_=mask_t[:, :], compare_op=ALU.is_ge, fill=NEG, base=0,
                                   pattern=[[1, P]], channel_multiplier=-1).then_inc(const_ok, 1)
                pool.affine_select(out=identb[:, :], in_=identb[:, :], compare_op=ALU.not_equal, fill=1.0,
                                   base=0, pattern=[[-1, P]], channel_multiplier=1).then_inc(const_ok, 1)

            @block.vector
            def _(dve):
                def unit(u, q):
                    if len(UNITS[u]) == 1:
                        return split(u, q, UNITS[u][0])
                    i, half, heads, width = UNITS[u]
                    dve.wait_ge(sc_ok, q * NU + u + 1)
                    r, a, nh = heads[0] % 2, heads[0] // 2, len(heads)
                    to = mx[0][:, 0:4 * HQ] if i < HQ else by_half[half][:, :]
                    to = to.rearrange("p (r a i) -> p r a i", r=2, a=2)[:, r, a:a + nh, i % HQ]
                    nc.vector.tensor_reduce(to, psc[u % 2][:, 0:nh * width].rearrange("p (h w) -> p h w", h=nh),
                                            AX.X, ALU.max).then_inc(mx_ok, 1)
                    if u == NU - 2:
                        dve.wait_ge(mx_ok, q * NU + u + 1)
                        nc.vector.tensor_tensor(mx[1][:, 0:4 * HQ], by_half[0][:, :], by_half[1][:, :],
                                                ALU.max).then_inc(mxb_ok, 1)

                def split(u, q, half):
                    dve.wait_ge(sc_ok, q * NU + u + 1)
                    if not isinstance(q, int):
                        dve.wait_ge(m_in[half], 16 * MLOADS * q)
                    turned = psc[u % 2][0:4 * HQ, 0:P]
                    nc.vector.tensor_scalar(mh[half][:, :], turned, -1.0, None, ALU.mult).then_inc(mstep, 1)
                    dve.wait_ge(mstep, q * 2 + half + 1 + clears)
                    nc.vector.scalar_tensor_tensor(out=ml[half][:, :], in0=turned, scalar=-1.0,
                                                   in1=mh[half][:, :].bitcast(F32), op0=ALU.mult,
                                                   op1=ALU.subtract).then_inc(mx_ok, 1)

                clears = 2
                for i in range(2):
                    nc.vector.memset(mx[i][:, :], 0.0).then_inc(mstep, 1)
                    nc.vector.memset(po[i][:, :], 0.0).then_inc(o_ok[i], 1)
                    nc.vector.memset(osb[i][:, :], 0.0).then_inc(o_out[i], 16)
                dve.wait_ge(mstep, clears)
                for u in range(NU):
                    unit(u, 0)
                with dve.Fori(0, QUADS // 2) as it:
                    for s in range(2):
                        for u in range(NU):
                            unit(u, 2 * it + s + 1)

            @block.scalar
            def _(act):
                with act.Fori(0, QUADS // 2) as it:
                    for s in range(2):
                        q = 2 * it + s
                        for n, (half, j, q0) in enumerate(STEPS):
                            width = (half + 1) * HALF - q0
                            for pair in range(2):
                                act.wait_ge(st_ok, q * 2 * NS + 2 * n + pair + 1)
                                nc.scalar.activation(pr[n % RING][:, 2 * pair:2 * pair + 2, 0:width],
                                                     pst[pair][:, :, 0:width], ACT.Exp, scale=SCALE).then_inc(ex_ok, 1)
                            if n == HQ:
                                output(nc, act, q, 0, it, s, pv_ok, o_out, o_ok, osb, po, NS)
                        output(nc, act, q, 1, it, s, pv_ok, o_out, o_ok, osb, po, NS)

            @block.tensor
            def _(pe):
                def unit(u, q, s):
                    if len(UNITS[u]) == 1:
                        pe.wait_ge(mx_ok, q * NU + u - 1)
                        if UNITS[u][0] == 1:
                            pe.wait_ge(mxb_ok, q + 1)
                        nc.tensor.transpose(psc[u % 2][:, 0:P], mx[UNITS[u][0]][:, :], k.ident[:, :]
                                            ).then_inc(sc_ok, 1)
                        return
                    i, half, heads, width = UNITS[u]
                    if u == 0:
                        pe.wait_ge(qa_in[s], count(q, s, LOADS))
                    if u == A_UNITS:
                        pe.wait_ge(qb_in[s], count(q, s, LOADS))
                    if not isinstance(q, int) or u >= 2:
                        pe.wait_ge(mx_ok, q * NU + u - 1)
                    diagonal = (i + 1) * P == half * HALF + width
                    for x, h in enumerate(heads):
                        a, r = h // 2, h % 2
                        rows = slice(64 * r, 64 * r + MROW)
                        out = psc[u % 2][:, x * width:(x + 1) * width]
                        last = nc.tensor.matmul(out, qs[s][rows, i // HQ, a, bass.ts(i % HQ, P)],
                                                ks[s][rows, half, a, 0:width],
                                                start=True, stop=not diagonal)
                        if diagonal:
                            last = nc.tensor.matmul(out[:, width - P:width], identb[:, :], mask[:, :],
                                                    start=False, stop=True)
                    last.then_inc(sc_ok, 1)

                def count(q, s, loads):
                    if isinstance(q, int):
                        return 32 * loads * (q // 2 + 1)
                    return q * (16 * loads) + (2 - s) * 16 * loads

                def scores(n, q, s):
                    half, j, q0 = STEPS[n]
                    width = (half + 1) * HALF - q0
                    if n == 0 or n == HQ:
                        pe.wait_ge(m_in[half], q * (16 * MLOADS) + 16 * MLOADS)
                    for pair in range(2):
                        if n > 0:
                            pe.wait_ge(ex_ok, q * (2 * NS) + 2 * n - 1 + pair)
                        for x in range(2):
                            h = 2 * pair + x
                            a, r = h // 2, h % 2
                            rows = slice(64 * r, 64 * r + KROWS)
                            last = nc.tensor.matmul(pst[pair][:, x, 0:width], ks[s][rows, j // HQ, a, bass.ts(j % HQ, P)],
                                                    qs[s][rows, half, a, HALF - width:HALF],
                                                    start=True, stop=q0 != j * P)
                            if q0 == j * P:
                                last = nc.tensor.matmul(pst[pair][:, x, 0:P], identb[:, :], mask_t[:, :],
                                                        start=False, stop=True)
                        last.then_inc(st_ok, 1)

                def values(n, q, s):
                    half, j, q0 = STEPS[n]
                    width = (half + 1) * HALF - q0
                    pe.wait_ge(ex_ok, q * (2 * NS) + 2 * n + 2)
                    if n == 0:
                        pe.wait_ge(v_in[s], (q - s) * 8 + 16)
                    if j == 0:
                        pe.wait_ge(o_ok[half], q + 1)
                    for h in range(4):
                        last = nc.tensor.matmul(po[half][32 * h:32 * h + ONES, q0 - half * HALF:HALF],
                                                vq[s][:, j, h, :], pr[n % RING][:, h, 0:width],
                                                start=j == 0, stop=j == HQ * (half + 1) - 1,
                                                tile_position=(0, 32 * h))
                    last.then_inc(pv_ok, 1)

                pe.wait_ge(const_ok, 3)
                pe.wait_ge(clear_ok, 4)
                for u in range(NU):
                    unit(u, 0, 0)

                def quad(q, s):
                    done = 0
                    scores(0, q, s)
                    for n in range(NS):
                        if n + 1 < NS:
                            scores(n + 1, q, s)
                        for u in range(done, per[n]):
                            unit(u, q + 1, 1 - s)
                        done = per[n]
                        values(n, q, s)

                with pe.Fori(0, QUADS // 2) as it:
                    for s in range(2):
                        quad(2 * it + s, s)


def output(nc, act, q, half, it, s, pv_ok, o_out, o_ok, osb, po, NS):
    act.wait_ge(pv_ok, q * NS + (HQ if half == 0 else NS))
    act.wait_ge(o_out[half], q * 16 + 16)
    nc.scalar.activation(osb[half][:, :], po[half][:, :], ACT.Copy).then_inc(o_ok[half], 1)


def project_phase(nc, d, k, src, dst):
    with ExitStack() as ctx:
        sb = lambda n, s, t: ctx.enter_context(nc.sbuf_tensor("o_" + n, s, t))
        ps = lambda n, s: ctx.enter_context(nc.psum_tensor("o_" + n, s, F32))
        sem = lambda n: ctx.enter_context(nc.semaphore("o_" + n))
        woh, wol = sb("woh", [P, KC, C], F32R), sb("wol", [P, KC, C], F32R)
        turn_weights(nc, k, [d["wo"]], [(woh, wol)], "to_")
        W = 2 * P
        NW = T // W
        on = [sb(f"on{i}", [P, KC, W], F32) for i in range(2)]
        sm = [sb(f"sm{i}", [P, KC, W], F32) for i in range(2)]
        oh = [sb(f"oh{i}", [P, KC, W], F32R) for i in range(2)]
        ol = [sb(f"ol{i}", [P, KC, W], F32R) for i in range(2)]
        res = [sb(f"res{i}", [P, C], F32) for i in range(4)]
        py = [ps(f"py{i}", [P, C]) for i in range(4)]
        o_in = [sem(f"o_in{i}") for i in range(2)]
        inv_ok, norm_ok, oh_ok, ol_ok = sem("inv_ok"), sem("norm_ok"), sem("oh_ok"), sem("ol_ok")
        y_ok, out_ok, stat_ok = sem("y_ok"), sem("out_ok"), sem("stat_ok")
        r_in = [sem(f"r_in{i}") for i in range(4)]
        stored = [sem(f"stored{i}") for i in range(4)]
        step, var_ok, std_ok = sem("step"), sem("var_ok"), sem("std_ok")
        NB = TOK // W
        with nc.Block() as block:
            @block.sync
            def _(sp):
                o5 = k.o.rearrange("(b g e h c) t -> b g e h c t", b=B, g=KC, e=2, h=4)
                for n in range(NB):
                    b, at = n // NW, slice(n % NW * W, (n % NW + 1) * W)
                    s = n % 2
                    if n >= 2:
                        sp.wait_ge(ol_ok, n - 1)
                    for g in range(KC):
                        for e in range(2):
                            for h in range(4):
                                row = (e * 4 + h) * D
                                sp.dma_start(on[s][row:row + D, g, :], o5[b, g, e, h, 0:D, at]).then_inc(o_in[s], 16)
                                sp.dma_start(sm[s][row:row + D, g, :],
                                             o5[b, g, e, h, D:D + 1, at].broadcast_to([D, W])).then_inc(o_in[s], 16)
                    for t in range(2):
                        m = 2 * n + t
                        if m >= 4:
                            sp.wait_ge(stored[m % 4], 16 * (m // 4))
                        sp.dma_start(res[m % 4][:, :], src[m * P:(m + 1) * P, :]).then_inc(r_in[m % 4], 16)

            @block.gpsimd
            def _(pool):
                for m in range(TILES):
                    pool.wait_ge(stat_ok, m + 1)
                    pool.dma_start(dst[m * P:(m + 1) * P, :], res[m % 4][:, :]).then_inc(stored[m % 4], 16)
                for i in range(4):
                    pool.wait_ge(stored[i], 16 * TILES // 4)

            @block.vector
            def _(dve):
                def normalise(n):
                    s = n % 2
                    dve.wait_ge(o_in[s], 16 * 16 * KC * (n // 2 + 1))
                    nc.vector.reciprocal(sm[s][:, :, :], sm[s][:, :, :]).then_inc(inv_ok, 1)
                    dve.wait_ge(inv_ok, n + 1)
                    nc.vector.tensor_tensor(on[s][:, :, :], on[s][:, :, :], sm[s][:, :, :], ALU.mult).then_inc(norm_ok, 1)
                    dve.wait_ge(oh_ok, n + 1)
                    nc.vector.tensor_tensor(ol[s][:, :, :], on[s][:, :, :], oh[s][:, :, :].bitcast(F32),
                                            ALU.subtract).then_inc(ol_ok, 1)

                normalise(0)
                for n in range(NB):
                    if n + 1 < NB:
                        normalise(n + 1)
                    for t in range(2):
                        m = 2 * n + t
                        dve.wait_ge(y_ok, m + 1)
                        dve.wait_ge(r_in[m % 4], 16 * (m // 4 + 1))
                        nc.vector.tensor_tensor(res[m % 4][:, :], res[m % 4][:, :], py[m % 4][:, :],
                                                ALU.add).then_inc(out_ok, 1)
                        dve.wait_ge(out_ok, m + 1)
                        nc.vector.bn_stats(k.stats[:, m, :], res[m % 4][:, :]).then_inc(stat_ok, 1)
                dve.wait_ge(stat_ok, TILES)
                layernorm_factors(nc, dve, k, step, var_ok, std_ok)

            @block.scalar
            def _(act):
                for n in range(NB):
                    act.wait_ge(norm_ok, n + 1)
                    if n >= 2:
                        act.wait_ge(y_ok, 2 * (n - 1))
                    nc.scalar.activation(oh[n % 2][:, :, :], on[n % 2][:, :, :], ACT.Copy).then_inc(oh_ok, 1)
                act.wait_ge(var_ok, 1)
                nc.scalar.activation(k.std[:, :], k.var[:, :], ACT.Sqrt).then_inc(std_ok, 1)

            @block.tensor
            def _(pe):
                for m in range(TILES):
                    s, t = m // 2 % 2, m % 2
                    pe.wait_ge(ol_ok, m // 2 + 1)
                    if m >= 4:
                        pe.wait_ge(out_ok, m - 3)
                    pairs = [(x[:, g, t * P:(t + 1) * P], w[:, g, :]) for g in range(KC)
                             for x, w in parts_of_product(oh[s], ol[s], woh, wol)]
                    for i, (x, w) in enumerate(pairs):
                        last = nc.tensor.matmul(py[m % 4][:, :], x, w, start=i == 0, stop=i == len(pairs) - 1)
                    last.then_inc(y_ok, 1)


class Kept:
    pass


def build(nc, d, out):
    k = Kept()
    scratch = lambda n, s: nc.dram_tensor(n, s, F32).ap()
    k.x1 = scratch("x1_scratch", (TOK, C))
    k.x2 = scratch("x2_scratch", (TOK, C))
    k.qh, k.ql, k.kh, k.kl = (scratch(n + "_scratch", (B * C, T)) for n in ("qh", "ql", "kh", "kl"))
    k.v = scratch("v_scratch", (QUADS, T, 4 * ONES))
    k.o = scratch("o_scratch", (QUADS * P, T))
    with ExitStack() as ctx:
        sb = lambda n, s, t: ctx.enter_context(nc.sbuf_tensor(n, s, t))
        k.w1h, k.w1l = sb("w1h", [P, KC, HID], F32R), sb("w1l", [P, KC, HID], F32R)
        k.w3h, k.w3l = sb("w3h", [P, KC, HID], F32R), sb("w3l", [P, KC, HID], F32R)
        k.w2h, k.w2l = sb("w2h", [P, HT, C], F32R), sb("w2l", [P, HT, C], F32R)
        k.ident = sb("ident", [P, P], F32)
        k.stats = sb("stats", [P, TILES, 6], F32)
        k.moments = sb("moments", [P, TILES, 2], F32)
        k.mean, k.var = sb("mean", [P, TILES], F32), sb("var", [P, TILES], F32)
        k.std, k.rstd = sb("std", [P, TILES], F32), sb("rstd", [P, TILES], F32)
        k.rope = sb("rope", [P, 3, QT], F32)
        weights_phase(nc, d, k)
        ffn_phase(nc, k, d["x"], k.x1, "f1_", True)
        qkv_phase(nc, d, k, k.x1)
        attention_phase(nc, k)
        project_phase(nc, d, k, k.x1, k.x2)
        ffn_phase(nc, k, k.x2, out, "f2_", False)


NAMES = {"x": "L0_attn_x", "wq": "L0_attn_wq", "wk": "L0_attn_wk", "wv": "L0_attn_wv", "wo": "L0_attn_wo",
         "w1": "L0_ffn_w1", "s1": "L0_ffn_s1", "w2": "L0_ffn_w2", "s2": "L0_ffn_s2", "w3": "L0_ffn_w3",
         "s3": "L0_ffn_s3"}


def rope_table():
    t = np.arange(T, dtype=np.float32).reshape(QT, P).T
    return np.ascontiguousarray(np.stack([np.cos(t), np.sin(t), -np.sin(t)], axis=1).astype(np.float32))


def kernel(**inputs):
    import numpy as _np
    import concourse.bacc as _bacc
    from concourse import mybir as _mybir
    from concourse.bass_utils import run_bass_kernel_spmd as _run

    nc = _bacc.Bacc("TRN2", target_bir_lowering=False, num_devices=1)
    arrays = {"in_" + n: _np.ascontiguousarray(inputs[full]) for n, full in NAMES.items()}
    arrays["in_x"] = arrays["in_x"].reshape(TOK, C)
    arrays["in_rope"] = rope_table()
    d = {n[3:]: nc.dram_tensor(n, a.shape, _mybir.dt.from_np(a.dtype), kind="ExternalInput").ap()
         for n, a in arrays.items()}
    out = nc.dram_tensor("out", (TOK, C), F32, kind="ExternalOutput").ap()
    build(nc, d, out)
    r = _run(nc, [arrays], core_ids=[0])
    return r.results[0]["out"].reshape(B, T, C)
```

```python
from contextlib import ExitStack

import numpy as np

import concourse.bass as bass
from concourse import mybir

F32 = mybir.dt.float32
F32R = mybir.dt.float32r
BF16 = mybir.dt.bfloat16
I32 = mybir.dt.int32
ALU = mybir.AluOpType
ACT = mybir.ActivationFunctionType
AX = mybir.AxisListType

P = 128
B, T, C = 2, 1024, 512
TOK = B * T
H, D = 32, 16
HID = 1376
GROUP = 64
KC = C // P
HT = -(-HID // P)
HLAST = HID - (HT - 1) * P
TILES = TOK // P
CHUNK = 512
CT = CHUNK // P
NCH = TOK // CHUNK
EPS = 1e-5
SCALE = D ** -0.5
NEG = -1e30
QUADS = B * H // 4
QT = T // P
ONES = D + 1
PARTS = 3


def hidden_rows(ht):
    return P if ht < HT - 1 else HLAST


def wait_alone(eng, sem, value, sure, least):
    value = eng.to_reg(value)
    eng.wait_ge(sure, least)
    eng.wait_ge(sem, value)


def parts_of_product(high_a, low_a, high_b, low_b):
    return ((high_a, high_b), (high_a, low_b), (low_a, high_b))


def weights_phase(nc, d, k):
    packs = [
        ("w1", k.w1h, k.w1l),
        ("w3", k.w3h, k.w3l),
        ("w2", k.w2h, k.w2l),
    ]
    RPP = 4 * HT
    R2 = HID * C // (2 * GROUP) // P
    BANKS = 6
    with ExitStack() as ctx:
        sb = lambda n, s, t: ctx.enter_context(nc.sbuf_tensor(n, s, t))
        sem = lambda n: ctx.enter_context(nc.semaphore(n))
        packed = [sb(f"packed{i}", [P, RPP, GROUP], I32) for i in range(2)]
        scales = [sb(f"scales{i}", [P, RPP, 2], F32) for i in range(3)]
        deq = [sb(f"deq{i}", [P, RPP, 2, GROUP], F32) for i in range(2)]
        xs = [sb(f"xs{i}", [P, C], F32) for i in range(2)]
        turned = [ctx.enter_context(nc.psum_tensor(f"wt{i}", [P, 4, P], F32)) for i in range(BANKS)]

        packed_in = [sem(f"w_packed_in{i}") for i in range(3)]
        unpacked = sem("w_unpacked")
        scaled = sem("w_scaled")
        step = sem("w_step")
        cleared = sem("w_cleared")
        turned_ok = sem("w_turned")
        high_ok = sem("w_high")
        low_ok = sem("w_low")
        ident_ok = sem("w_ident")
        ident_z = sem("w_ident_zero")
        x_in = [sem(f"w_x_in{i}") for i in range(2)]
        x_seen = sem("w_x_seen")
        var_ok = sem("w_var")
        std_ok = sem("w_std")
        rope_in = sem("w_rope_in")

        def source(w, g):
            flat = deq[w % 2][:, :, :, :].rearrange("p r s c -> p (r s c)")
            if w < 2:
                n = hidden_rows(g)
                return [flat[0:n, g * C + c * P:g * C + (c + 1) * P] for c in range(KC)], P, n
            n = hidden_rows(g)
            return [flat[:, b * HID + g * P:b * HID + g * P + n] for b in range(4)], n, P

        def target(w, g, part):
            if w < 2:
                return part[:, :, g * P:g * P + hidden_rows(g)]
            return part[0:hidden_rows(g), g, :].rearrange("h (p b) -> h b p", b=4)

        def bank(w, g):
            _, rows, cols = source(w, g)
            return turned[(w * HT + g) % BANKS][0:rows, :, 0:cols]

        with nc.Block() as block:
            @block.sync
            def _(sp):
                for w, (name, _, _) in enumerate(packs):
                    src, sc = d[name], d["s" + name[1]]
                    if w >= 2:
                        sp.wait_ge(unpacked, w - 1)
                    if w < 2:
                        full = (HT - 1) * P
                        sp.wait_ge(cleared, 4)
                        sp.dma_start(packed[w][:, 0:4 * (HT - 1), :].rearrange("p (t r) c -> p t (r c)", r=4),
                                     src[0:4 * full, :].rearrange("(t p r) c -> p t (r c)", p=P, r=4)
                                     ).then_inc(packed_in[w], 16)
                        sp.dma_start(packed[w][0:HLAST, 4 * (HT - 1):RPP, :].rearrange("p r c -> p (r c)"),
                                     src[4 * full:4 * HID, :].rearrange("(p r) c -> p (r c)", r=4)
                                     ).then_inc(packed_in[w], 16)
                        sp.dma_start(scales[w][:, 0:4 * (HT - 1), :].rearrange("p (t r) s -> p t (r s)", r=4),
                                     sc[0:8 * full].rearrange("(t p g) -> p t g", p=P, g=8)
                                     ).then_inc(packed_in[w], 16)
                        sp.dma_start(scales[w][0:HLAST, 4 * (HT - 1):RPP, :].rearrange("p r s -> p (r s)"),
                                     sc[8 * full:8 * HID].rearrange("(p g) -> p g", g=8)
                                     ).then_inc(packed_in[w], 16)
                    else:
                        sp.dma_start(packed[w % 2][:, 0:R2, :].rearrange("p r c -> p (r c)"),
                                     src.rearrange("(p r) c -> p (r c)", p=P)).then_inc(packed_in[w], 16)
                        sp.dma_start(scales[w][:, 0:R2, :].rearrange("p r s -> p (r s)"),
                                     sc.rearrange("(p g) -> p g", p=P)).then_inc(packed_in[w], 16)

            @block.gpsimd
            def _(pool):
                for w in range(2):
                    pool.memset(packed[w][:, 4 * (HT - 1):RPP, :], 0).then_inc(cleared, 1)
                    pool.memset(scales[w][:, 4 * (HT - 1):RPP, :], 0.0).then_inc(cleared, 1)
                pool.memset(k.ident[:, :], 0.0).then_inc(ident_z, 1)
                pool.wait_ge(ident_z, 1)
                pool.affine_select(out=k.ident[:, :], in_=k.ident[:, :], compare_op=ALU.not_equal, fill=1.0,
                                   base=0, pattern=[[-1, P]], channel_multiplier=1).then_inc(ident_ok, 1)
                pool.dma_start(k.rope[:, :, :], d["rope"]).then_inc(rope_in, 16)
                for t in range(TILES):
                    if t >= 2:
                        pool.wait_ge(x_seen, t - 1)
                    pool.dma_start(xs[t % 2][:, :], d["x"][t * P:(t + 1) * P, :]).then_inc(x_in[t % 2], 16)
                pool.wait_ge(rope_in, 16)

            @block.vector
            def _(dve):
                steps = [0]

                def unpack(w):
                    rows = RPP if w < 2 else R2
                    src, out = packed[w % 2][:, 0:rows, :], deq[w % 2][:, 0:rows, :, :]
                    bits = out.bitcast(I32)
                    dve.wait_ge(packed_in[w], 64 if w < 2 else 32)
                    if w >= 2:
                        dve.wait_ge(low_ok, (w - 1) * HT)
                    nc.vector.tensor_scalar(bits[:, :, 0, :], src, 4, None, ALU.arith_shift_right)
                    nc.vector.tensor_scalar(bits[:, :, 1, :], src, 15, 8, ALU.bitwise_and,
                                            ALU.bitwise_xor).then_inc(unpacked, 1)
                    dve.wait_ge(unpacked, w + 1)
                    for s in range(2):
                        by = scales[w][:, 0:rows, s:s + 1].broadcast_to([P, rows, GROUP])
                        nc.vector.scalar_tensor_tensor(out=out[:, :, s, :], in0=bits[:, :, s, :],
                                                       scalar=-8.0 * s, in1=by, op0=ALU.add,
                                                       op1=ALU.mult).then_inc(scaled, 1)

                seen = [0]

                def see():
                    t = seen[0]
                    if t < TILES:
                        dve.wait_ge(x_in[t % 2], 16 * (t // 2 + 1))
                        nc.vector.bn_stats(k.stats[:, t, :], xs[t % 2][:, :]).then_inc(x_seen, 1)
                        seen[0] += 1

                def low_parts(w):
                    for g in range(HT):
                        see()
                        dve.wait_ge(high_ok, w * HT + g + 1)
                        nc.vector.tensor_tensor(target(w, g, packs[w][2]), bank(w, g),
                                                target(w, g, packs[w][1]).bitcast(F32),
                                                ALU.subtract).then_inc(low_ok, 1)

                unpack(0)
                unpack(1)
                low_parts(0)
                unpack(2)
                low_parts(1)
                low_parts(2)
                dve.wait_ge(x_seen, TILES)
                layernorm_factors(nc, dve, k, step, var_ok, std_ok)

            @block.scalar
            def _(act):
                for w in range(3):
                    for g in range(HT):
                        act.wait_ge(turned_ok, w * HT + g + 1)
                        nc.scalar.activation(target(w, g, packs[w][1]), bank(w, g), ACT.Copy).then_inc(high_ok, 1)
                act.wait_ge(var_ok, 1)
                nc.scalar.activation(k.std[:, :], k.var[:, :], ACT.Sqrt).then_inc(std_ok, 1)

            @block.tensor
            def _(pe):
                pe.wait_ge(ident_ok, 1)
                for w in range(3):
                    pe.wait_ge(scaled, 2 * (w + 1))
                    for g in range(HT):
                        n = w * HT + g
                        if n >= BANKS:
                            pe.wait_ge(low_ok, n - BANKS + 1)
                        blocks, rows, cols = source(w, g)
                        for b, blk in enumerate(blocks):
                            at = turned[n % BANKS][0:rows, b, 0:cols]
                            last = nc.tensor.transpose(at, blk, k.ident[0:blk.shape[0], 0:blk.shape[0]])
                        last.then_inc(turned_ok, 1)


def layernorm_factors(nc, dve, k, step, var_ok, std_ok):
    for t in range(TILES):
        last = nc.vector.bn_aggr(k.moments[:, t, :], k.stats[:, t, :])
    last.then_inc(step, 1)
    dve.wait_ge(step, 1)
    nc.vector.tensor_scalar(k.var[:, :], k.moments[:, :, 1], EPS, None, ALU.add).then_inc(var_ok, 1)
    nc.vector.tensor_copy(k.mean[:, :], k.moments[:, :, 0])
    dve.wait_ge(std_ok, 1)
    nc.vector.reciprocal(k.rstd[:, :], k.std[:, :]).then_inc(step, 1)
    dve.wait_ge(step, 2)


def ffn_phase(nc, k, src, dst, tag, stats):
    with ExitStack() as ctx:
        sb = lambda n, s, t: ctx.enter_context(nc.sbuf_tensor(tag + n, s, t))
        ps = lambda n, s: ctx.enter_context(nc.psum_tensor(tag + n, s, F32))
        sem = lambda n: ctx.enter_context(nc.semaphore(tag + n))
        xnh = sb("xnh", [P, KC, CHUNK], F32R)
        xnl = sb("xnl", [P, KC, CHUNK], F32R)
        gh = sb("gh", [P, HT, CHUNK], F32R)
        gl = sb("gl", [P, HT, CHUNK], F32R)
        xr = [sb(f"xr{i}", [P, C], F32) for i in range(2)]
        sa = [sb(f"sa{i}", [P, CHUNK], F32) for i in range(2)]
        g32 = [sb(f"g{i}", [P, CHUNK], F32) for i in range(2)]
        res = [sb(f"res{i}", [P, C], F32) for i in range(2)]
        pa = [ps(f"pa{i}", [P, CHUNK]) for i in range(2)]
        pb = [ps(f"pb{i}", [P, CHUNK]) for i in range(2)]
        pt = [ps(f"pt{i}", [P, KC, P]) for i in range(2)]
        py = [ps(f"py{i}", [P, C]) for i in range(2)]

        x_in = [sem(f"x_in{i}") for i in range(2)]
        xn_ok = sem("xn_ok")
        xt_ok = sem("xt_ok")
        xh_ok = sem("xh_ok")
        xl_ok = sem("xl_ok")
        ab_ok = sem("ab_ok")
        sa_ok = sem("sa_ok")
        g_ok = sem("g_ok")
        gh_ok = sem("gh_ok")
        gl_ok = sem("gl_ok")
        y_ok = sem("y_ok")
        r_in = [sem(f"r_in{i}") for i in range(2)]
        out_ok = sem("out_ok")
        stat_ok = sem("stat_ok")
        stored = [sem(f"stored{i}") for i in range(2)]
        step, var_ok, std_ok = sem("step"), sem("var_ok"), sem("std_ok")
        w2_out = sem("w2_out")

        def rows(n):
            return src[bass.ds((n & (TILES - 1)) * P, P), :] if not isinstance(n, int) else src[n * P:(n + 1) * P, :]

        with nc.Block() as block:
            @block.sync
            def _(sp):
                for t in range(2):
                    sp.dma_start(xr[t][:, :], rows(t)).then_inc(x_in[t], 16)
                for t in range(2, CT):
                    sp.wait_ge(xt_ok, t - 1)
                    sp.dma_start(xr[t % 2][:, :], rows(t)).then_inc(x_in[t % 2], 16)
                for t in range(2):
                    sp.dma_start(res[t][:, :], rows(t)).then_inc(r_in[t], 16)

                def load_next(c, t):
                    wait_alone(sp, xt_ok, c * CT + CT + t - 1, x_in[0], 16)
                    sp.dma_start(xr[t % 2][:, :], rows(c * CT + CT + t)).then_inc(x_in[t % 2], 16)

                def store(c, t):
                    wait_alone(sp, stat_ok, c * CT + t + 1, x_in[0], 16)
                    sp.dma_start(dst[bass.ds((c * CT + t) * P, P), :], res[t % 2][:, :]).then_inc(stored[t % 2], 16)

                def load_residual(c, t):
                    wait_alone(sp, stored[t % 2], c * 32 + (t // 2 + 1) * 16, x_in[0], 16)
                    sp.dma_start(res[t % 2][:, :], rows(c * CT + t + 2)).then_inc(r_in[t % 2], 16)

                with sp.Fori(0, NCH) as c:
                    load_next(c, 0)
                    load_next(c, 1)
                    load_next(c, 2)
                    store(c, 0)
                    load_residual(c, 0)
                    load_next(c, 3)
                    for t in range(1, CT):
                        store(c, t)
                        load_residual(c, t)
                for i in range(2):
                    sp.wait_ge(stored[i], 16 * TILES // 2)
                    sp.wait_ge(r_in[i], 16 * (TILES // 2 + 1))
                    sp.wait_ge(x_in[i], 16 * (TILES + CT) // 2)

            @block.vector
            def _(dve):
                def normalise(n, t, k_in):
                    dve.wait_ge(x_in[t % 2], k_in)
                    at = (n & (TILES - 1)) if not isinstance(n, int) else n
                    nc.vector.tensor_scalar(xr[t % 2][:, :], xr[t % 2][:, :], k.mean[:, bass.ds(at, 1)],
                                            k.rstd[:, bass.ds(at, 1)], ALU.subtract, ALU.mult).then_inc(xn_ok, 1)

                def low_part(n, t):
                    dve.wait_ge(xh_ok, n + 1)
                    at = slice(t * P, (t + 1) * P)
                    nc.vector.tensor_tensor(xnl[:, :, at], pt[t % 2][:, :, :], xnh[:, :, at].bitcast(F32),
                                            ALU.subtract).then_inc(xl_ok, 1)

                for t in range(CT):
                    normalise(t, t, 16 * (t // 2 + 1))
                    low_part(t, t)

                with dve.Fori(0, NCH) as c:
                    for ht in range(HT):
                        n = hidden_rows(ht)
                        dve.wait_ge(sa_ok, c * HT + ht + 1)
                        if ht >= 2:
                            dve.wait_ge(gl_ok, c * HT + ht - 1)
                        nc.vector.tensor_tensor(g32[ht % 2][0:n, :], sa[ht % 2][0:n, :], pb[ht % 2][0:n, :],
                                                ALU.mult).then_inc(g_ok, 1)
                        if ht in (4, 6):
                            t = (ht - 4) // 2
                            normalise(c * CT + CT + t, t, c * 32 + 48)
                    for t in range(CT):
                        low_part(c * CT + CT + t, t)
                        if t < 2:
                            normalise(c * CT + CT + t + 2, t, c * 32 + 64)
                        dve.wait_ge(y_ok, c * CT + t + 1)
                        dve.wait_ge(r_in[t % 2], c * 32 + (t // 2 + 1) * 16)
                        nc.vector.scalar_tensor_tensor(out=res[t % 2][:, :], in0=py[t % 2][:, :], scalar=0.5,
                                                       in1=res[t % 2][:, :], op0=ALU.mult,
                                                       op1=ALU.add).then_inc(out_ok, 1)
                        dve.wait_ge(out_ok, c * CT + t + 1)
                        if stats:
                            nc.vector.bn_stats(k.stats[:, bass.ds(c * CT + t, 1), :].rearrange("p a s -> p (a s)"),
                                               res[t % 2][:, :]).then_inc(stat_ok, 1)
                        else:
                            dve.sem_inc(stat_ok, 1)
                if stats:
                    dve.wait_ge(stat_ok, TILES)
                    layernorm_factors(nc, dve, k, step, var_ok, std_ok)

            @block.scalar
            def _(act):
                def high_part(n, t):
                    act.wait_ge(xt_ok, n + 1)
                    if isinstance(n, int) and n >= 2:
                        act.wait_ge(xl_ok, n - 1)
                    nc.scalar.activation(xnh[:, :, t * P:(t + 1) * P], pt[t % 2][:, :, :], ACT.Copy).then_inc(xh_ok, 1)

                for t in range(CT):
                    high_part(t, t)
                with act.Fori(0, NCH) as c:
                    for ht in range(HT):
                        n = hidden_rows(ht)
                        act.wait_ge(ab_ok, c * HT + ht + 1)
                        if ht >= 2:
                            act.wait_ge(g_ok, c * HT + ht - 1)
                        nc.scalar.activation(sa[ht % 2][0:n, :], pa[ht % 2][0:n, :], ACT.Silu).then_inc(sa_ok, 1)
                        act.wait_ge(g_ok, c * HT + ht + 1)
                        nc.scalar.activation(gh[0:n, ht, :], g32[ht % 2][0:n, :], ACT.Copy).then_inc(gh_ok, 1)
                    for t in range(CT):
                        high_part(c * CT + CT + t, t)
                if stats:
                    act.wait_ge(var_ok, 1)
                    nc.scalar.activation(k.std[:, :], k.var[:, :], ACT.Sqrt).then_inc(std_ok, 1)

            @block.gpsimd
            def _(pool):
                if stats:
                    for part, to in zip((k.w2h, k.w2l), k.w2_parts):
                        for r, t in ((P, slice(0, HT - 1)), (HLAST, slice(HT - 1, HT))):
                            pool.dma_start(to[0:r, t, :], part[0:r, t, :].bitcast(F32)).then_inc(w2_out, 16)
                with pool.Fori(0, NCH) as c:
                    for ht in range(HT):
                        n = hidden_rows(ht)
                        pool.wait_ge(gh_ok, c * HT + ht + 1)
                        nc.gpsimd.tensor_tensor(gl[0:n, ht, :], g32[ht % 2][0:n, :], gh[0:n, ht, :].bitcast(F32),
                                                ALU.subtract).then_inc(gl_ok, 1)
                if stats:
                    pool.wait_ge(w2_out, 64)

            @block.tensor
            def _(pe):
                def turn(n, t):
                    pe.wait_ge(xn_ok, n + 1)
                    if not isinstance(n, int) or n >= 2:
                        pe.wait_ge(xl_ok, n - 1)
                    for c4 in range(KC):
                        last = nc.tensor.transpose(pt[t % 2][:, c4, :], xr[t % 2][:, c4 * P:(c4 + 1) * P],
                                                   k.ident[:, :])
                    last.then_inc(xt_ok, 1)

                def product(out, wh, wl, ht):
                    n = hidden_rows(ht)
                    pairs = [(w[:, c4, ht * P:ht * P + n], x[:, c4, :])
                             for c4 in range(KC) for w, x in parts_of_product(wh, wl, xnh, xnl)]
                    for i, (w, x) in enumerate(pairs):
                        last = nc.tensor.matmul(out, w, x, start=i == 0, stop=i == len(pairs) - 1)
                    return last

                for t in range(CT):
                    turn(t, t)
                with pe.Fori(0, NCH) as c:
                    pe.wait_ge(xl_ok, c * CT + CT)
                    for ht in range(HT):
                        n = hidden_rows(ht)
                        if ht >= 2:
                            pe.wait_ge(g_ok, c * HT + ht - 1)
                        product(pa[ht % 2][0:n, :], k.w1h, k.w1l, ht)
                        product(pb[ht % 2][0:n, :], k.w3h, k.w3l, ht).then_inc(ab_ok, 1)
                    for t in range(CT):
                        turn(c * CT + CT + t, t)
                        if t >= 2:
                            pe.wait_ge(out_ok, c * CT + t - 1)
                        for ht in range(HT):
                            n = hidden_rows(ht)
                            if t == 0:
                                pe.wait_ge(gl_ok, c * HT + ht + 1)
                            at = slice(t * P, (t + 1) * P)
                            for i, (g, w) in enumerate(parts_of_product(gh, gl, k.w2h, k.w2l)):
                                last = nc.tensor.matmul(py[t % 2][:, :], g[0:n, ht, at], w[0:n, ht, :],
                                                        start=ht == 0 and i == 0, stop=ht == HT - 1 and i == 2)
                        last.then_inc(y_ok, 1)


def turn_weights(nc, k, sources, parts, tag):
    with ExitStack() as ctx:
        nat = [ctx.enter_context(nc.sbuf_tensor(f"{tag}nat{i}", [P, KC, C], F32)) for i in range(2)]
        pt = [ctx.enter_context(nc.psum_tensor(f"{tag}pt{i}", [P, C], F32)) for i in range(4)]
        sem = lambda n: ctx.enter_context(nc.semaphore(tag + n))
        w_in, turned, high, low = [sem(f"w_in{i}") for i in range(2)], sem("turned"), sem("high"), sem("low")
        n_w = len(sources)
        with nc.Block() as block:
            @block.sync
            def _(sp):
                for w in range(n_w):
                    if w >= 2:
                        sp.wait_ge(turned, KC * (w - 1))
                    sp.dma_start(nat[w % 2][:, :, :], sources[w].rearrange("(o p) i -> p o i", p=P)
                                 ).then_inc(w_in[w % 2], 16)

            @block.tensor
            def _(pe):
                for w in range(n_w):
                    pe.wait_ge(w_in[w % 2], 16 * (w // 2 + 1))
                    for c4 in range(KC):
                        n = w * KC + c4
                        if n >= 4:
                            pe.wait_ge(low, n - 3)
                        for o in range(KC):
                            last = nc.tensor.transpose(pt[n % 4][:, o * P:(o + 1) * P],
                                                       nat[w % 2][:, o, c4 * P:(c4 + 1) * P], k.ident[:, :])
                        last.then_inc(turned, 1)

            @block.scalar
            def _(act):
                for n in range(n_w * KC):
                    act.wait_ge(turned, n + 1)
                    nc.scalar.activation(parts[n // KC][0][:, n % KC, :], pt[n % 4][:, :], ACT.Copy).then_inc(high, 1)

            @block.vector
            def _(dve):
                for n in range(n_w * KC):
                    dve.wait_ge(high, n + 1)
                    nc.vector.tensor_tensor(parts[n // KC][1][:, n % KC, :], pt[n % 4][:, :],
                                            parts[n // KC][0][:, n % KC, :].bitcast(F32),
                                            ALU.subtract).then_inc(low, 1)


def qkv_phase(nc, d, k, src):
    with ExitStack() as ctx:
        sb = lambda n, s, t: ctx.enter_context(nc.sbuf_tensor(n, s, t))
        ps = lambda n, s: ctx.enter_context(nc.psum_tensor(n, s, F32))
        sem = lambda n: ctx.enter_context(nc.semaphore("q_" + n))
        parts = [(sb(f"{w}h", [P, KC, C], F32R), sb(f"{w}l", [P, KC, C], F32R)) for w in ("wq", "wk", "wv")]
        turn_weights(nc, k, [d["wq"], d["wk"], d["wv"]], parts, "tq_")

        xr = [sb(f"qxr{i}", [P, C], F32) for i in range(2)]
        xh = [sb(f"qxh{i}", [P, KC, P], F32R) for i in range(2)]
        xl = [sb(f"qxl{i}", [P, KC, P], F32R) for i in range(2)]
        turn = [sb(f"turn{i}", [P, 3], F32) for i in range(2)]
        by_cos = sb("by_cos", [P, C], F32)
        roped = [sb(f"roped{i}", [P, C], F32) for i in range(2)]
        th = [sb(f"th{i}", [P, KC, P], F32R) for i in range(2)]
        tl = [sb(f"tl{i}", [P, KC, P], F32R) for i in range(2)]
        va = sb("va", [P, H, ONES], F32)
        pt = ps("q_pt", [P, KC, P])
        pj = [ps(f"q_pj{i}", [P, C]) for i in range(3)]
        pr = [ps(f"q_pr{i}", [P, KC, P]) for i in range(2)]

        x_in = [sem(f"x_in{i}") for i in range(2)]
        xn_ok, xt_ok, xh_ok, xl_ok = sem("xn_ok"), sem("xt_ok"), sem("xh_ok"), sem("xl_ok")
        pj_ok = [sem(f"pj_ok{i}") for i in range(3)]
        cos_ok = [sem(f"cos_ok{i}") for i in range(2)]
        rope_ok = [sem(f"rope_ok{i}") for i in range(2)]
        v_ok = sem("v_ok")
        rt_ok = [sem(f"rt_ok{i}") for i in range(2)]
        th_ok = [sem(f"th_ok{i}") for i in range(2)]
        tl_ok = [sem(f"tl_ok{i}") for i in range(2)]
        th_out = [sem(f"th_out{i}") for i in range(2)]
        tl_out = [sem(f"tl_out{i}") for i in range(2)]
        v_out = sem("v_out")
        ones_ok = sem("ones_ok")

        def rows(n):
            return src[bass.ds((n & (TILES - 1)) * P, P), :] if not isinstance(n, int) else src[n * P:(n + 1) * P, :]

        with nc.Block() as block:
            @block.sync
            def _(sp):
                for t in range(2):
                    sp.dma_start(xr[t][:, :], rows(t)).then_inc(x_in[t], 16)
                for b in range(B):
                    with sp.Fori(0, QT // 2) as j:
                        i = j + b * (QT // 2)
                        for s in range(2):
                            wait_alone(sp, xt_ok, 2 * i + s + 1, x_in[0], 16)
                            sp.dma_start(xr[s][:, :], rows(2 * i + s + 2)).then_inc(x_in[s], 16)
                            toks = bass.ds((2 * j + s) * P, P)
                            rowsb = slice(b * C, (b + 1) * C)
                            for m, (hi, lo) in enumerate(((k.qh, k.ql), (k.kh, k.kl))):
                                wait_alone(sp, th_ok[m], 2 * i + s + 1, x_in[0], 16)
                                sp.dma_start(hi[rowsb, toks].rearrange("(g p) q -> p g q", p=P),
                                             th[m][:, :, :].bitcast(F32)).then_inc(th_out[m], 16)
                                wait_alone(sp, tl_ok[m], 2 * i + s + 1, x_in[0], 16)
                                sp.dma_start(lo[rowsb, toks].rearrange("(g p) q -> p g q", p=P),
                                             tl[m][:, :, :].bitcast(F32)).then_inc(tl_out[m], 16)
                            wait_alone(sp, v_ok, 2 * i + s + 1, x_in[0], 16)
                            sp.dma_start(k.v[b * (H // 4):(b + 1) * (H // 4), toks, :].rearrange("a q c -> q a c"),
                                         va[:, :, :].rearrange("p (a h) c -> p a (h c)", h=4)).then_inc(v_out, 16)
                for m in range(2):
                    sp.wait_ge(th_out[m], 16 * TILES)
                    sp.wait_ge(tl_out[m], 16 * TILES)
                    sp.wait_ge(x_in[m], 16 * (TILES // 2 + 1))
                sp.wait_ge(v_out, 16 * TILES)

            @block.gpsimd
            def _(pool):
                pool.memset(va[:, :, :], 1.0).then_inc(ones_ok, 1)

            @block.vector
            def _(dve):
                def normalise(n, s, count):
                    dve.wait_ge(x_in[s], count)
                    at = (n & (TILES - 1)) if not isinstance(n, int) else n
                    nc.vector.tensor_scalar(xr[s][:, :], xr[s][:, :], k.mean[:, bass.ds(at, 1)],
                                            k.rstd[:, bass.ds(at, 1)], ALU.subtract, ALU.mult).then_inc(xn_ok, 1)

                def low_x(n, s):
                    dve.wait_ge(xh_ok, n + 1)
                    nc.vector.tensor_tensor(xl[s][:, :, :], pt[:, :, :], xh[s][:, :, :].bitcast(F32),
                                            ALU.subtract).then_inc(xl_ok, 1)

                def angles(n, s):
                    at = (n & (QT - 1)) if not isinstance(n, int) else n
                    nc.vector.tensor_copy(turn[s][:, :].unsqueeze(2), k.rope[:, :, bass.ds(at, 1)])

                def rotate(n, s, m):
                    dve.wait_ge(cos_ok[m], n + 1)
                    pairs = lambda a: a[:, :].rearrange("p (h two) -> p h two", two=2)
                    x, c, o = pairs(pj[m]), pairs(by_cos), pairs(roped[m])
                    nc.vector.scalar_tensor_tensor(out=o[:, :, 0], in0=x[:, :, 1], scalar=turn[s][:, 2:3],
                                                   in1=c[:, :, 0], op0=ALU.mult, op1=ALU.add)
                    nc.vector.scalar_tensor_tensor(out=o[:, :, 1], in0=x[:, :, 0], scalar=turn[s][:, 1:2],
                                                   in1=c[:, :, 1], op0=ALU.mult, op1=ALU.add).then_inc(rope_ok[m], 1)

                def low_t(n, m, first):
                    dve.wait_ge(th_ok[m], n + 1)
                    if not first:
                        dve.wait_ge(tl_out[m], 16 * n)
                    nc.vector.tensor_tensor(tl[m][:, :, :], pr[m][:, :, :], th[m][:, :, :].bitcast(F32),
                                            ALU.subtract).then_inc(tl_ok[m], 1)

                def tile(n, s, count, first=False):
                    rotate(n, s, 0)
                    low_x(n + 1, 1 - s)
                    normalise(n + 2, s, count)
                    rotate(n, s, 1)
                    dve.wait_ge(rope_ok[1], n + 1)
                    angles(n + 2, s)
                    low_t(n, 0, first)
                    low_t(n, 1, first)

                angles(0, 0)
                angles(1, 1)
                normalise(0, 0, 16)
                normalise(1, 1, 16)
                low_x(0, 0)
                tile(0, 0, 32, True)
                tile(1, 1, 32)
                with dve.Fori(1, TILES // 2) as i:
                    for s in range(2):
                        tile(2 * i + s, s, i * 16 + 32)

            @block.scalar
            def _(act):
                def high_x(n, s):
                    act.wait_ge(xt_ok, n + 1)
                    nc.scalar.activation(xh[s][:, :, :], pt[:, :, :], ACT.Copy).then_inc(xh_ok, 1)

                def cos_part(n, s, m, first):
                    act.wait_ge(pj_ok[m], n + 1)
                    if m == 1:
                        act.wait_ge(rope_ok[0], n + 1)
                    elif not first:
                        act.wait_ge(rope_ok[1], n)
                    nc.scalar.activation(by_cos[:, :], pj[m][:, :], ACT.Copy,
                                         scale=turn[s][:, 0:1]).then_inc(cos_ok[m], 1)

                def tile(n, s, first=False):
                    cos_part(n, s, 0, first)
                    high_x(n + 1, 1 - s)
                    cos_part(n, s, 1, first)
                    act.wait_ge(pj_ok[2], n + 1)
                    if not first:
                        act.wait_ge(v_out, 16 * n)
                    nc.scalar.activation(va[:, :, 0:D], pj[2][:, :].rearrange("p (h c) -> p h c", c=D),
                                         ACT.Copy).then_inc(v_ok, 1)
                    for m in range(2):
                        act.wait_ge(rt_ok[m], n + 1)
                        if not first:
                            act.wait_ge(th_out[m], 16 * n)
                        nc.scalar.activation(th[m][:, :, :], pr[m][:, :, :], ACT.Copy).then_inc(th_ok[m], 1)

                high_x(0, 0)
                act.wait_ge(ones_ok, 1)
                tile(0, 0, True)
                tile(1, 1)
                with act.Fori(1, TILES // 2) as i:
                    for s in range(2):
                        tile(2 * i + s, s)

            @block.tensor
            def _(pe):
                def turn_x(n, s):
                    pe.wait_ge(xn_ok, n + 1)
                    for c4 in range(KC):
                        last = nc.tensor.transpose(pt[:, c4, :], xr[s][:, c4 * P:(c4 + 1) * P], k.ident[:, :])
                    last.then_inc(xt_ok, 1)

                def project(m, s):
                    pairs = [(x[:, c4, :], w[:, c4, :]) for c4 in range(KC)
                             for x, w in parts_of_product(xh[s], xl[s], *parts[m])]
                    for i, (x, w) in enumerate(pairs):
                        last = nc.tensor.matmul(pj[m][:, :], x, w, start=i == 0, stop=i == len(pairs) - 1)
                    last.then_inc(pj_ok[m], 1)

                def tile(n, s, first=False):
                    pe.wait_ge(xl_ok, n + 1)
                    if not first:
                        pe.wait_ge(rope_ok[0], n)
                    project(0, s)
                    turn_x(n + 1, 1 - s)
                    if not first:
                        pe.wait_ge(rope_ok[1], n)
                    project(1, s)
                    if not first:
                        pe.wait_ge(v_ok, n)
                    project(2, s)
                    for m in range(2):
                        pe.wait_ge(rope_ok[m], n + 1)
                        if not first:
                            pe.wait_ge(tl_ok[m], n)
                        for c4 in range(KC):
                            last = nc.tensor.transpose(pr[m][:, c4, :], roped[m][:, c4 * P:(c4 + 1) * P],
                                                       k.ident[:, :])
                        last.then_inc(rt_ok[m], 1)

                turn_x(0, 0)
                tile(0, 0, True)
                tile(1, 1)
                with pe.Fori(1, TILES // 2) as i:
                    for s in range(2):
                        tile(2 * i + s, s)


HALF = T // 2
HQ = QT // 2
PARTS = 4
PLAIN = PARTS * D + 1
MROW = PLAIN
KROWS = MROW + 2


def score_units():
    units = []
    for i in range(QT):
        for half in range(i // HQ + 1):
            width = min(HALF, (i + 1) * P - half * HALF)
            together = HALF // width
            for h in range(0, 4, together):
                units.append((i, half, range(h, min(h + together, 4)), width))
    first = sum(1 for u in units if u[0] < HQ)
    units.insert(first + 3, (0,))
    units.append((1,))
    return units


def attention_steps():
    return [(half, j, max(half * HALF, j * P)) for half in range(2) for j in range(HQ * (half + 1))]


def attention_phase(nc, k):
    UNITS, STEPS = score_units(), attention_steps()
    NU, NS = len(UNITS), len(STEPS)
    A_UNITS = sum(1 for u in UNITS if len(u) > 1 and u[0] < HQ)
    BATCH = 2
    RING = 2 * BATCH
    assert NS % RING == 0 and HQ % BATCH == 0
    LOADS = 2 * PARTS
    with ExitStack() as ctx:
        sb = lambda n, s, t: ctx.enter_context(nc.sbuf_tensor("a_" + n, s, t))
        ps = lambda n, s: ctx.enter_context(nc.psum_tensor("a_" + n, s, F32))
        sem = lambda n: ctx.enter_context(nc.semaphore("a_" + n))
        qs = [sb(f"qs{i}", [P, 2, 4, HALF], F32R) for i in range(2)]
        ks = [sb(f"ks{i}", [P, 2, 4, HALF], F32R) for i in range(2)]
        vq = [sb(f"vq{i}", [P, QT, 4, ONES], F32) for i in range(2)]
        pr = [sb(f"probs{i}", [P, 4, HALF], F32) for i in range(RING)]
        osb = [sb(f"osb{i}", [P, HALF], F32) for i in range(2)]
        mx = [sb(f"rowmax{i}", [P, P], F32) for i in range(2)]
        by_half = [sb(f"max_half{i}", [P, 4 * HQ], F32) for i in range(2)]
        mh = [sb(f"mh{i}", [4 * HQ, P], F32R) for i in range(2)]
        ml = [sb(f"ml{i}", [4 * HQ, P], F32R) for i in range(2)]
        mask = sb("mask", [P, P], BF16)
        mask_t = sb("mask_t", [P, P], BF16)
        identb = sb("identb", [P, P], BF16)
        psc = [ps(f"psc{i}", [P, HALF]) for i in range(2)]
        pst = [ps(f"pst{i}", [P, 2, HALF]) for i in range(2)]
        po = [ps(f"po{i}", [P, HALF]) for i in range(2)]

        const_z, const_ok, clear_ok = sem("const_z"), sem("const_ok"), sem("clear_ok")
        qk_in = [[sem(f"qk_in{i}{half}") for half in range(2)] for i in range(2)]
        v_in = [sem(f"v_in{i}") for i in range(2)]
        sc_ok = sem("sc_ok")
        mx_ok = sem("mx_ok")
        mxb_ok = sem("mxb_ok")
        mstep = sem("mstep")
        m_in = [sem(f"m_in{i}") for i in range(2)]
        st_ok = sem("st_ok")
        ex_ok = sem("ex_ok")
        pv_ok = sem("pv_ok")
        o_ok = [sem(f"o_ok{i}") for i in range(2)]
        o_out = [sem(f"o_out{i}") for i in range(2)]
        osb_ok = sem("osb_ok")

        def quads(eng):
            with eng.Fori(0, QUADS // 2 - 1) as it:
                yield 2 * it, 0
                yield 2 * it + 1, 1
            yield QUADS - 2, 0
            yield QUADS - 1, 1

        def more(q, ahead):
            return not isinstance(q, int) or q + ahead < QUADS

        def loaded(q, s, dmas):
            return (q - s) * (8 * dmas) + 16 * dmas

        with nc.Block() as block:
            @block.sync
            def _(sp):
                def load(q, s, half):
                    at = slice(half * HALF, (half + 1) * HALF)
                    for stack, scratches in ((qs[s], (k.qh, k.qh, k.ql, k.ql)), (ks[s], (k.kh, k.kl, k.kh, k.kl))):
                        for part, scratch in enumerate(scratches):
                            src = scratch[bass.ds(q * (4 * D), 4 * D), at].rearrange("(h d) t -> d h t", d=D)
                            sp.dma_start(stack[part * D:(part + 1) * D, half, :, :].bitcast(F32), src
                                         ).then_inc(qk_in[s][half], 16)

                def put_max(q, s, half):
                    sp.wait_ge(mx_ok, q * NU + UNITS.index((half,)) + 1)
                    for x, m in enumerate((mh[half], ml[half])):
                        sp.dma_start(qs[s][MROW + x:MROW + x + 1, half, :, :].rearrange("o h t -> o (h t)").bitcast(F32),
                                     m[:, :].bitcast(F32)).then_inc(m_in[half], 16)

                for half in range(2):
                    load(0, 0, half)
                for half in range(2):
                    load(1, 1, half)
                sp.wait_ge(clear_ok, 4)
                put_max(0, 0, 0)
                put_max(0, 0, 1)
                for q, s in quads(sp):
                    if more(q, 1):
                        put_max(q + 1, 1 - s, 0)
                    if more(q, 2):
                        wait_alone(sp, pv_ok, q * NS + 2 * HQ, qk_in[0][0], 16)
                        load(q + 2, s, 0)
                        wait_alone(sp, pv_ok, q * NS + NS, qk_in[0][0], 16)
                        load(q + 2, s, 1)
                    if more(q, 1):
                        put_max(q + 1, 1 - s, 1)
                for i in range(2):
                    sp.wait_ge(m_in[i], 32 * QUADS)

            @block.gpsimd
            def _(pool):
                def load_v(q, s):
                    pool.dma_start(vq[s][:, :, :, :].rearrange("p j h c -> p j (h c)"),
                                   k.v[bass.ds(q, 1), :, :].rearrange("o (j p) c -> p (o j) c", p=P)
                                   ).then_inc(v_in[s], 16)

                pool.memset(mask[:, :], 0.0).then_inc(const_z, 1)
                pool.memset(mask_t[:, :], 0.0).then_inc(const_z, 1)
                pool.memset(identb[:, :], 0.0).then_inc(const_z, 1)
                pool.wait_ge(const_z, 3)
                pool.affine_select(out=mask[:, :], in_=mask[:, :], compare_op=ALU.is_ge, fill=NEG, base=0,
                                   pattern=[[-1, P]], channel_multiplier=1).then_inc(const_ok, 1)
                pool.affine_select(out=mask_t[:, :], in_=mask_t[:, :], compare_op=ALU.is_ge, fill=NEG, base=0,
                                   pattern=[[1, P]], channel_multiplier=-1).then_inc(const_ok, 1)
                pool.affine_select(out=identb[:, :], in_=identb[:, :], compare_op=ALU.not_equal, fill=1.0,
                                   base=0, pattern=[[-1, P]], channel_multiplier=1).then_inc(const_ok, 1)
                for s in range(2):
                    load_v(s, s)
                pool.wait_ge(osb_ok, 2)
                for half in range(2):
                    pool.dma_start(k.o[0:P, half * HALF:(half + 1) * HALF], osb[half][:, :]).then_inc(o_out[half], 16)
                for q, s in quads(pool):
                    for half in range(2):
                        wait_alone(pool, o_ok[half], q + 2, const_ok, 3)
                        pool.dma_start(k.o[bass.ds(q * P, P), half * HALF:(half + 1) * HALF],
                                       osb[half][:, :]).then_inc(o_out[half], 16)
                    if more(q, 2):
                        load_v(q + 2, s)
                for i in range(2):
                    pool.wait_ge(o_out[i], 16 * (QUADS + 1))

            @block.vector
            def _(dve):
                def unit(u, q):
                    if len(UNITS[u]) == 1:
                        return split(u, q, UNITS[u][0])
                    i, half, heads, width = UNITS[u]
                    dve.wait_ge(sc_ok, q * NU + u + 1)
                    nh = len(heads)
                    to = mx[0][:, 0:4 * HQ] if i < HQ else by_half[half][:, :]
                    to = to.rearrange("p (h i) -> p h i", h=4)[:, heads[0]:heads[0] + nh, i % HQ]
                    nc.vector.tensor_reduce(to, psc[u % 2][:, 0:nh * width].rearrange("p (h w) -> p h w", h=nh),
                                            AX.X, ALU.max).then_inc(mx_ok, 1)
                    if u == NU - 2:
                        dve.wait_ge(mx_ok, q * NU + u + 1)
                        nc.vector.tensor_tensor(mx[1][:, 0:4 * HQ], by_half[0][:, :], by_half[1][:, :],
                                                ALU.max).then_inc(mxb_ok, 1)

                def split(u, q, half):
                    dve.wait_ge(sc_ok, q * NU + u + 1)
                    if not isinstance(q, int) or q > 0:
                        dve.wait_ge(m_in[half], 32 * q)
                    turned = psc[u % 2][0:4 * HQ, 0:P]
                    nc.vector.tensor_scalar(mh[half][:, :], turned, -1.0, None, ALU.mult).then_inc(mstep, 1)
                    dve.wait_ge(mstep, q * 2 + half + 1 + clears)
                    nc.vector.scalar_tensor_tensor(out=ml[half][:, :], in0=turned, scalar=-1.0,
                                                   in1=mh[half][:, :].bitcast(F32), op0=ALU.mult,
                                                   op1=ALU.subtract).then_inc(mx_ok, 1)

                clears = 2
                for s in range(2):
                    nc.vector.memset(qs[s][64:96, :, :, :].bitcast(F32), 0.0).then_inc(clear_ok, 1)
                    nc.vector.memset(ks[s][64:96, :, :, :].bitcast(F32), 1.0).then_inc(clear_ok, 1)
                for i in range(2):
                    nc.vector.memset(mx[i][:, :], 0.0).then_inc(mstep, 1)
                    nc.vector.memset(po[i][:, :], 0.0).then_inc(o_ok[i], 1)
                    nc.vector.memset(osb[i][:, :], 0.0).then_inc(osb_ok, 1)
                dve.wait_ge(mstep, clears)
                for u in range(NU):
                    unit(u, 0)
                for q, s in quads(dve):
                    if more(q, 1):
                        for u in range(NU):
                            unit(u, q + 1)

            @block.scalar
            def _(act):
                def exps(n, q):
                    half, j, q0 = STEPS[n]
                    width = (half + 1) * HALF - q0
                    for pair in range(2):
                        act.wait_ge(st_ok, q * (2 * NS) + 2 * n + pair + 1)
                        nc.scalar.activation(pr[n % RING][:, 2 * pair:2 * pair + 2, 0:width],
                                             pst[pair][:, :, 0:width], ACT.Exp, scale=SCALE).then_inc(ex_ok, 1)

                def output(half, q):
                    act.wait_ge(pv_ok, q * NS + (HQ if half == 0 else NS))
                    act.wait_ge(o_out[half], q * 16 + 16)
                    nc.scalar.activation(osb[half][:, :], po[half][:, :], ACT.Copy).then_inc(o_ok[half], 1)

                for n in range(BATCH):
                    exps(n, 0)
                for q, s in quads(act):
                    for n in range(BATCH, NS):
                        exps(n, q)
                        if n == HQ + BATCH - 1:
                            output(0, q)
                    if more(q, 1):
                        for n in range(BATCH):
                            exps(n, q + 1)
                    output(1, q)

            @block.tensor
            def _(pe):
                def unit(u, q, s):
                    if u >= 2 or not isinstance(q, int) or q > 0:
                        pe.wait_ge(mx_ok, q * NU + u - 1)
                    if len(UNITS[u]) == 1:
                        if UNITS[u][0] == 1:
                            pe.wait_ge(mxb_ok, q + 1)
                        nc.tensor.transpose(psc[u % 2][:, 0:P], mx[UNITS[u][0]][:, :], k.ident[:, :]
                                            ).then_inc(sc_ok, 1)
                        return
                    i, half, heads, width = UNITS[u]
                    if u == 0:
                        pe.wait_ge(qk_in[s][0], loaded(q, s, LOADS))
                    if u == A_UNITS:
                        pe.wait_ge(qk_in[s][1], loaded(q, s, LOADS))
                    diagonal = (i + 1) * P == half * HALF + width
                    for x, h in enumerate(heads):
                        out = psc[u % 2][:, x * width:(x + 1) * width]
                        last = nc.tensor.matmul(out, qs[s][0:PLAIN, i // HQ, h, bass.ts(i % HQ, P)],
                                                ks[s][0:PLAIN, half, h, 0:width], start=True, stop=not diagonal)
                        if diagonal:
                            last = nc.tensor.matmul(out[:, width - P:width], identb[:, :], mask[:, :],
                                                    start=False, stop=True)
                    last.then_inc(sc_ok, 1)

                def scores(n, q, s, pair):
                    half, j, q0 = STEPS[n]
                    width = (half + 1) * HALF - q0
                    if j == 0 and pair == 0:
                        pe.wait_ge(m_in[half], q * 32 + 32)
                    if n > 0 or not isinstance(q, int) or q > 0:
                        pe.wait_ge(ex_ok, q * (2 * NS) + 2 * n - 1 + pair)
                    for x in range(2):
                        h = 2 * pair + x
                        last = nc.tensor.matmul(pst[pair][:, x, 0:width], ks[s][0:KROWS, j // HQ, h, bass.ts(j % HQ, P)],
                                                qs[s][0:KROWS, half, h, HALF - width:HALF],
                                                start=True, stop=q0 != j * P)
                        if q0 == j * P:
                            last = nc.tensor.matmul(pst[pair][:, x, 0:P], identb[:, :], mask_t[:, :],
                                                    start=False, stop=True)
                    last.then_inc(st_ok, 1)

                def values(n, q, s):
                    half, j, q0 = STEPS[n]
                    width = (half + 1) * HALF - q0
                    pe.wait_ge(ex_ok, q * (2 * NS) + 2 * n + 2)
                    if n == 0:
                        pe.wait_ge(v_in[s], loaded(q, s, 1))
                    if j == 0:
                        pe.wait_ge(o_ok[half], q + 1)
                    for h in range(4):
                        last = nc.tensor.matmul(po[half][32 * h:32 * h + ONES, q0 - half * HALF:HALF],
                                                vq[s][:, j, h, :], pr[n % RING][:, h, 0:width],
                                                start=j == 0, stop=j == HQ * (half + 1) - 1,
                                                tile_position=(0, 32 * h))
                    last.then_inc(pv_ok, 1)

                def quad(q, s):
                    done = 0
                    for n0 in range(0, NS, BATCH):
                        slots = 2 * BATCH
                        for x in range(slots):
                            n, pair = n0 + BATCH + x // 2, x % 2
                            if n < NS:
                                scores(n, q, s, pair)
                            elif more(q, 1):
                                scores(n - NS, q + 1, 1 - s, pair)
                            upto = ((NU - 1) * (slots * (n0 // BATCH) + x + 1) // (slots * (NS // BATCH) - 1))
                            upto = NU if n0 + BATCH == NS and x == slots - 1 else min(upto, NU - 1)
                            for u in range(done, upto):
                                if more(q, 1):
                                    unit(u, q + 1, 1 - s)
                            done = upto
                        for n in range(n0, n0 + BATCH):
                            values(n, q, s)

                pe.wait_ge(const_ok, 3)
                pe.wait_ge(clear_ok, 4)
                for u in range(NU):
                    unit(u, 0, 0)
                for n in range(BATCH):
                    for pair in range(2):
                        scores(n, 0, 0, pair)
                for q, s in quads(pe):
                    quad(q, s)


def project_phase(nc, d, k, src, dst):
    with ExitStack() as ctx:
        sb = lambda n, s, t: ctx.enter_context(nc.sbuf_tensor("o_" + n, s, t))
        ps = lambda n, s: ctx.enter_context(nc.psum_tensor("o_" + n, s, F32))
        sem = lambda n: ctx.enter_context(nc.semaphore("o_" + n))
        woh, wol = sb("woh", [P, KC, C], F32R), sb("wol", [P, KC, C], F32R)
        W = 2 * P
        NW = T // W
        NB = TOK // W
        NH = B * H
        HH = T // 2
        sums = sb("sums", [P, HH], F32)
        nat = sb("nat", [P, KC, C], F32)
        on = [sb(f"on{i}", [P, KC, W], F32) for i in range(2)]
        sm = [sb(f"sm{i}", [P, KC, W], F32) for i in range(2)]
        oh = [sb(f"oh{i}", [P, KC, W], F32R) for i in range(2)]
        ol = [sb(f"ol{i}", [P, KC, W], F32R) for i in range(2)]
        res = [sb(f"res{i}", [P, C], F32) for i in range(4)]
        pt = [ps(f"pt{i}", [P, C]) for i in range(4)]
        py = [ps(f"py{i}", [P, C]) for i in range(4)]
        sums_in, inverted, inv_out = sem("sums_in"), sem("inverted"), sem("inv_out")
        w_in, turned, high, low = sem("w_in"), sem("turned"), sem("high"), sem("low")
        o_in = [sem(f"o_in{i}") for i in range(2)]
        norm_ok, oh_ok, ol_ok = sem("norm_ok"), sem("oh_ok"), sem("ol_ok")
        y_ok, out_ok, stat_ok = sem("y_ok"), sem("out_ok"), sem("stat_ok")
        r_in = [sem(f"r_in{i}") for i in range(4)]
        stored = [sem(f"stored{i}") for i in range(4)]
        step, var_ok, std_ok = sem("step"), sem("var_ok"), sem("std_ok")
        w2_in = sem("w2_in")
        o4 = k.o.rearrange("(q h r) t -> q h r t", h=4, r=32)
        with nc.Block() as block:
            @block.sync
            def _(sp):
                for x in range(2):
                    sp.dma_start(sums[x * NH:(x + 1) * NH, :], o4[:, :, D, x * HH:(x + 1) * HH]
                                 .rearrange("q h t -> (q h) t")).then_inc(sums_in, 16)
                sp.dma_start(nat[:, :, :], d["wo"].rearrange("(o p) i -> p o i", p=P)).then_inc(w_in, 16)
                sp.wait_ge(inverted, 1)
                for x in range(2):
                    sp.dma_start(k.inverse[:, :, x * HH:(x + 1) * HH].rearrange("q h t -> (q h) t"),
                                 sums[x * NH:(x + 1) * NH, :]).then_inc(inv_out, 16)
                sp.wait_ge(inv_out, 32)
                for n in range(NB):
                    b, at = n // NW, slice(n % NW * W, (n % NW + 1) * W)
                    s = n % 2
                    if n >= 2:
                        sp.wait_ge(ol_ok, n - 1)
                    for g in range(KC):
                        q = b * (H // 4) + 2 * g
                        sp.dma_start(on[s][:, g, :], o4[q:q + 2, :, 0:D, at].rearrange("q h r t -> (q h) r t")
                                     ).then_inc(o_in[s], 16)
                        sp.dma_start(sm[s][:, g, :], k.inverse[q:q + 2, :, at].rearrange("q h t -> (q h) t")
                                     .unsqueeze(1).broadcast_to([8, D, W])).then_inc(o_in[s], 16)
                    for t in range(2):
                        m = 2 * n + t
                        if m >= 4:
                            sp.wait_ge(stored[m % 4], 16 * (m // 4))
                        sp.dma_start(res[m % 4][:, :], src[m * P:(m + 1) * P, :]).then_inc(r_in[m % 4], 16)

            @block.gpsimd
            def _(pool):
                for m in range(TILES):
                    pool.wait_ge(stat_ok, m + 1)
                    pool.dma_start(dst[m * P:(m + 1) * P, :], res[m % 4][:, :]).then_inc(stored[m % 4], 16)
                for i in range(4):
                    pool.wait_ge(stored[i], 16 * TILES // 4)

            @block.vector
            def _(dve):
                dve.wait_ge(sums_in, 32)
                nc.vector.reciprocal(sums[:, :], sums[:, :]).then_inc(inverted, 1)
                for c4 in range(KC):
                    dve.wait_ge(high, c4 + 1)
                    nc.vector.tensor_tensor(wol[:, c4, :], pt[c4][:, :], woh[:, c4, :].bitcast(F32),
                                            ALU.subtract).then_inc(low, 1)

                def normalise(n):
                    s = n % 2
                    dve.wait_ge(o_in[s], 16 * 2 * KC * (n // 2 + 1))
                    nc.vector.tensor_tensor(on[s][:, :, :], on[s][:, :, :], sm[s][:, :, :], ALU.mult).then_inc(norm_ok, 1)
                    dve.wait_ge(oh_ok, n + 1)
                    nc.vector.tensor_tensor(ol[s][:, :, :], on[s][:, :, :], oh[s][:, :, :].bitcast(F32),
                                            ALU.subtract).then_inc(ol_ok, 1)

                normalise(0)
                for n in range(NB):
                    if n + 1 < NB:
                        normalise(n + 1)
                    for t in range(2):
                        m = 2 * n + t
                        dve.wait_ge(y_ok, m + 1)
                        dve.wait_ge(r_in[m % 4], 16 * (m // 4 + 1))
                        nc.vector.tensor_tensor(res[m % 4][:, :], res[m % 4][:, :], py[m % 4][:, :],
                                                ALU.add).then_inc(out_ok, 1)
                        dve.wait_ge(out_ok, m + 1)
                        nc.vector.bn_stats(k.stats[:, m, :], res[m % 4][:, :]).then_inc(stat_ok, 1)
                dve.wait_ge(stat_ok, TILES)
                layernorm_factors(nc, dve, k, step, var_ok, std_ok)

            @block.scalar
            def _(act):
                for part, src_ in zip((k.w2h, k.w2l), k.w2_parts):
                    for r, t in ((P, slice(0, HT - 1)), (HLAST, slice(HT - 1, HT))):
                        act.dma_start(part[0:r, t, :].bitcast(F32), src_[0:r, t, :]).then_inc(w2_in, 16)
                for c4 in range(KC):
                    act.wait_ge(turned, c4 + 1)
                    nc.scalar.activation(woh[:, c4, :], pt[c4][:, :], ACT.Copy).then_inc(high, 1)
                for n in range(NB):
                    act.wait_ge(norm_ok, n + 1)
                    if n >= 2:
                        act.wait_ge(y_ok, 2 * (n - 1))
                    nc.scalar.activation(oh[n % 2][:, :, :], on[n % 2][:, :, :], ACT.Copy).then_inc(oh_ok, 1)
                act.wait_ge(var_ok, 1)
                nc.scalar.activation(k.std[:, :], k.var[:, :], ACT.Sqrt).then_inc(std_ok, 1)
                act.wait_ge(w2_in, 64)

            @block.tensor
            def _(pe):
                pe.wait_ge(w_in, 16)
                for c4 in range(KC):
                    for o in range(KC):
                        last = nc.tensor.transpose(pt[c4][:, o * P:(o + 1) * P], nat[:, o, c4 * P:(c4 + 1) * P],
                                                   k.ident[:, :])
                    last.then_inc(turned, 1)
                pe.wait_ge(low, KC)
                for m in range(TILES):
                    s, t = m // 2 % 2, m % 2
                    pe.wait_ge(ol_ok, m // 2 + 1)
                    if m >= 4:
                        pe.wait_ge(out_ok, m - 3)
                    pairs = [(x[:, g, t * P:(t + 1) * P], w[:, g, :]) for g in range(KC)
                             for x, w in parts_of_product(oh[s], ol[s], woh, wol)]
                    for i, (x, w) in enumerate(pairs):
                        last = nc.tensor.matmul(py[m % 4][:, :], x, w, start=i == 0, stop=i == len(pairs) - 1)
                    last.then_inc(y_ok, 1)


class Kept:
    pass


def build(nc, d, out):
    k = Kept()
    scratch = lambda n, s: nc.dram_tensor(n, s, F32).ap()
    k.x1 = scratch("x1_scratch", (TOK, C))
    k.x2 = scratch("x2_scratch", (TOK, C))
    k.qh, k.ql, k.kh, k.kl = (scratch(n + "_scratch", (B * C, T)) for n in ("qh", "ql", "kh", "kl"))
    k.v = scratch("v_scratch", (QUADS, T, 4 * ONES))
    k.o = scratch("o_scratch", (QUADS * P, T))
    k.inverse = scratch("inverse_scratch", (QUADS, 4, T))
    k.w2_parts = [scratch(n + "_scratch", (P, HT, C)) for n in ("w2h", "w2l")]
    with ExitStack() as ctx:
        sb = lambda n, s, t: ctx.enter_context(nc.sbuf_tensor(n, s, t))
        k.w1h, k.w1l = sb("w1h", [P, KC, HID], F32R), sb("w1l", [P, KC, HID], F32R)
        k.w3h, k.w3l = sb("w3h", [P, KC, HID], F32R), sb("w3l", [P, KC, HID], F32R)
        k.ident = sb("ident", [P, P], F32)
        k.stats = sb("stats", [P, TILES, 6], F32)
        k.moments = sb("moments", [P, TILES, 2], F32)
        k.mean, k.var = sb("mean", [P, TILES], F32), sb("var", [P, TILES], F32)
        k.std, k.rstd = sb("std", [P, TILES], F32), sb("rstd", [P, TILES], F32)
        k.rope = sb("rope", [P, 3, QT], F32)
        with ExitStack() as w2:
            k.w2h, k.w2l = [w2.enter_context(nc.sbuf_tensor(n, [P, HT, C], F32R)) for n in ("w2h", "w2l")]
            weights_phase(nc, d, k)
            ffn_phase(nc, k, d["x"], k.x1, "f1_", True)
        qkv_phase(nc, d, k, k.x1)
        attention_phase(nc, k)
        with ExitStack() as w2:
            k.w2h, k.w2l = [w2.enter_context(nc.sbuf_tensor(n, [P, HT, C], F32R)) for n in ("w2h_again", "w2l_again")]
            project_phase(nc, d, k, k.x1, k.x2)
            ffn_phase(nc, k, k.x2, out, "f2_", False)


NAMES = {"x": "L0_attn_x", "wq": "L0_attn_wq", "wk": "L0_attn_wk", "wv": "L0_attn_wv", "wo": "L0_attn_wo",
         "w1": "L0_ffn_w1", "s1": "L0_ffn_s1", "w2": "L0_ffn_w2", "s2": "L0_ffn_s2", "w3": "L0_ffn_w3",
         "s3": "L0_ffn_s3"}


def rope_table():
    t = np.arange(T, dtype=np.float32).reshape(QT, P).T
    return np.ascontiguousarray(np.stack([np.cos(t), np.sin(t), -np.sin(t)], axis=1).astype(np.float32))


def kernel(**inputs):
    import numpy as _np
    import concourse.bacc as _bacc
    from concourse import mybir as _mybir
    from concourse.bass_utils import run_bass_kernel_spmd as _run

    nc = _bacc.Bacc("TRN2", target_bir_lowering=False, num_devices=1)
    arrays = {"in_" + n: _np.ascontiguousarray(inputs[full]) for n, full in NAMES.items()}
    arrays["in_x"] = arrays["in_x"].reshape(TOK, C)
    arrays["in_rope"] = rope_table()
    d = {n[3:]: nc.dram_tensor(n, a.shape, _mybir.dt.from_np(a.dtype), kind="ExternalInput").ap()
         for n, a in arrays.items()}
    out = nc.dram_tensor("out", (TOK, C), F32, kind="ExternalOutput").ap()
    build(nc, d, out)
    r = _run(nc, [arrays], core_ids=[0])
    return r.results[0]["out"].reshape(B, T, C)
```

```python
from contextlib import ExitStack

import numpy as np

import concourse.bass as bass
from concourse import mybir

F32 = mybir.dt.float32
F32R = mybir.dt.float32r
BF16 = mybir.dt.bfloat16
I32 = mybir.dt.int32
ALU = mybir.AluOpType
ACT = mybir.ActivationFunctionType
AX = mybir.AxisListType

P = 128
B, T, C = 2, 1024, 512
TOK = B * T
H, D = 32, 16
HID = 1376
GROUP = 64
KC = C // P
HT = -(-HID // P)
HLAST = HID - (HT - 1) * P
TILES = TOK // P
CHUNK = 512
CT = CHUNK // P
NCH = TOK // CHUNK
EPS = 1e-5
SCALE = D ** -0.5
NEG = -1e30
QUADS = B * H // 4
QT = T // P
ONES = D + 1
HALF = T // 2


def hidden_rows(ht):
    return P if ht < HT - 1 else HLAST


def wait_alone(eng, sem, value, sure, least):
    value = eng.to_reg(value)
    eng.wait_ge(sure, least)
    eng.wait_ge(sem, value)


def parts_of_product(high_a, low_a, high_b, low_b):
    return ((high_a, high_b), (high_a, low_b), (low_a, high_b))


def weights_phase(nc, d, k):
    packs = [
        ("w1", k.w1h, k.w1l),
        ("w3", k.w3h, k.w3l),
        ("w2", k.w2h, k.w2l),
    ]
    RPP = 4 * HT
    R2 = HID * C // (2 * GROUP) // P
    BANKS = 6
    with ExitStack() as ctx:
        sb = lambda n, s, t: ctx.enter_context(nc.sbuf_tensor(n, s, t))
        sem = lambda n: ctx.enter_context(nc.semaphore(n))
        packed = [sb(f"packed{i}", [P, RPP, GROUP], I32) for i in range(2)]
        scales = [sb(f"scales{i}", [P, RPP, 2], F32) for i in range(3)]
        deq = [sb(f"deq{i}", [P, RPP, 2, GROUP], F32) for i in range(2)]
        XR = 2
        xs = [sb(f"xs{i}", [P, C], F32) for i in range(XR)]
        whole = [sb(f"whole{i}", [P, 4, P], F32) for i in range(2)]
        turned = [ctx.enter_context(nc.psum_tensor(f"wt{i}", [P, 4, P], F32)) for i in range(BANKS)]

        packed_in = [sem(f"w_packed_in{i}") for i in range(3)]
        unpacked = sem("w_unpacked")
        odd_bits_ok = sem("w_odd_bits")
        odd_float_ok = sem("w_odd_float")
        even_ok = sem("w_even_ok")
        odd_ok = sem("w_odd_ok")
        step = sem("w_step")
        cleared = sem("w_cleared")
        turned_ok = sem("w_turned")
        high_ok = sem("w_high")
        whole_ok = sem("w_whole")
        low_ok = sem("w_low")
        odd_low_ok = sem("w_odd_low")
        ident_ok = sem("w_ident")
        ident_z = sem("w_ident_zero")
        table_ok = sem("w_table_ok")
        x_in = [sem(f"w_x_in{i}") for i in range(XR)]
        x_seen = sem("w_x_seen")
        var_ok = sem("w_var")
        std_ok = sem("w_std")
        rope_in = sem("w_rope_in")

        def scaled_groups(w, s):
            rows = RPP if w < 2 else R2
            out = deq[w % 2][:, 0:rows, s, :]
            return out.bitcast(I32), scales[w][:, 0:rows, s:s + 1].broadcast_to([P, rows, GROUP]), out

        def source(w, g):
            flat = deq[w % 2][:, :, :, :].rearrange("p r s c -> p (r s c)")
            if w < 2:
                n = hidden_rows(g)
                return [flat[0:n, g * C + c * P:g * C + (c + 1) * P] for c in range(KC)], P, n
            n = hidden_rows(g)
            return [flat[:, b * HID + g * P:b * HID + g * P + n] for b in range(4)], n, P

        def target(w, g, part):
            if w < 2:
                return part[:, :, g * P:g * P + hidden_rows(g)]
            return part[0:hidden_rows(g), g, :].rearrange("h (p b) -> h b p", b=4)

        def bank(w, g):
            _, rows, cols = source(w, g)
            return turned[(w * HT + g) % BANKS][0:rows, :, 0:cols]

        def banks(w, odd):
            return [(w * HT + g, w, g) for g in range(HT) if (w * HT + g) % 2 == odd]

        def whole_of(n, w, g):
            _, rows, cols = source(w, g)
            return whole[n // 2 % 2][0:rows, :, 0:cols]

        with nc.Block() as block:
            @block.sync
            def _(sp):
                def load_x(first, end):
                    for t in range(first, end):
                        if t >= XR:
                            sp.wait_ge(x_seen, t - XR + 1)
                        sp.dma_start(xs[t % XR][:, :], d["x"][t * P:(t + 1) * P, :]).then_inc(x_in[t % XR], 16)

                for w, (name, _, _) in enumerate(packs):
                    src, sc = d[name], d["s" + name[1]]
                    if w >= 2:
                        sp.wait_ge(unpacked, w - 1)
                    if w < 2:
                        full = (HT - 1) * P
                        sp.wait_ge(cleared, 4)
                        sp.dma_start(packed[w][:, 0:4 * (HT - 1), :].rearrange("p (t r) c -> p t (r c)", r=4),
                                     src[0:4 * full, :].rearrange("(t p r) c -> p t (r c)", p=P, r=4)
                                     ).then_inc(packed_in[w], 16)
                        sp.dma_start(packed[w][0:HLAST, 4 * (HT - 1):RPP, :].rearrange("p r c -> p (r c)"),
                                     src[4 * full:4 * HID, :].rearrange("(p r) c -> p (r c)", r=4)
                                     ).then_inc(packed_in[w], 16)
                        sp.dma_start(scales[w][:, 0:4 * (HT - 1), :].rearrange("p (t r) s -> p t (r s)", r=4),
                                     sc[0:8 * full].rearrange("(t p g) -> p t g", p=P, g=8)
                                     ).then_inc(packed_in[w], 16)
                        sp.dma_start(scales[w][0:HLAST, 4 * (HT - 1):RPP, :].rearrange("p r s -> p (r s)"),
                                     sc[8 * full:8 * HID].rearrange("(p g) -> p g", g=8)
                                     ).then_inc(packed_in[w], 16)
                    else:
                        sp.dma_start(packed[w % 2][:, 0:R2, :].rearrange("p r c -> p (r c)"),
                                     src.rearrange("(p r) c -> p (r c)", p=P)).then_inc(packed_in[w], 16)
                        sp.dma_start(scales[w][:, 0:R2, :].rearrange("p r s -> p (r s)"),
                                     sc.rearrange("(p g) -> p g", p=P)).then_inc(packed_in[w], 16)

                load_x(0, TILES)

            @block.gpsimd
            def _(pool):
                for w in range(2):
                    pool.memset(packed[w][:, 4 * (HT - 1):RPP, :], 0).then_inc(cleared, 1)
                    pool.memset(scales[w][:, 4 * (HT - 1):RPP, :], 0.0).then_inc(cleared, 1)
                pool.memset(k.ident[:, :], 0.0).then_inc(ident_z, 1)
                pool.memset(k.table_in[:, :], 1.0).then_inc(table_ok, 1)
                pool.wait_ge(ident_z, 1)
                pool.affine_select(out=k.ident[:, :], in_=k.ident[:, :], compare_op=ALU.not_equal, fill=1.0,
                                   base=0, pattern=[[-1, P]], channel_multiplier=1).then_inc(ident_ok, 1)
                pool.dma_start(k.rope[:, :, :], d["rope"]).then_inc(rope_in, 16)
                def scale(w):
                    pool.wait_ge(odd_float_ok, w + 1)
                    _, by, out = scaled_groups(w, 1)
                    nc.gpsimd.tensor_tensor(out, out, by, ALU.mult).then_inc(odd_ok, 1)

                def low_parts(w):
                    for n, w, g in banks(w, 1):
                        pool.wait_ge(whole_ok, n // 2 + 1)
                        nc.gpsimd.tensor_tensor(target(w, g, packs[w][2]), whole_of(n, w, g),
                                                target(w, g, packs[w][1]).bitcast(F32),
                                                ALU.subtract).then_inc(odd_low_ok, 1)

                scale(0)
                scale(1)
                low_parts(0)
                scale(2)
                low_parts(1)
                low_parts(2)
                pool.wait_ge(rope_in, 16)

            @block.vector
            def _(dve):
                steps = [0]

                def unpack(w):
                    src, bits = packed[w % 2][:, :, :], deq[w % 2][:, :, :, :].bitcast(I32)
                    high_bits, low_bits = bits[:, :, 0, :], bits[:, :, 1, :]
                    even_bits, by, out = scaled_groups(w, 0)
                    dve.wait_ge(packed_in[w], 64 if w < 2 else 32)
                    if w >= 2:
                        dve.wait_ge(turned_ok, (w - 1) * HT)
                    nc.vector.tensor_scalar(low_bits, src, 28, 28, ALU.logical_shift_left, ALU.arith_shift_right
                                            ).then_inc(odd_bits_ok, 1)
                    nc.vector.tensor_scalar(high_bits, src, 4, None, ALU.arith_shift_right).then_inc(unpacked, 1)
                    dve.wait_ge(unpacked, w + 1)
                    nc.vector.tensor_tensor(out, even_bits, by, ALU.mult).then_inc(even_ok, 1)

                seen = [0]

                def see():
                    t = seen[0]
                    if t < TILES:
                        dve.wait_ge(x_in[t % XR], 16 * (t // XR + 1))
                        nc.vector.bn_stats(k.stats[:, t, :], xs[t % XR][:, :]).then_inc(x_seen, 1)
                        seen[0] += 1

                def low_parts(w):
                    for n, w, g in banks(w, 0):
                        for _ in range(2):
                            see()
                        dve.wait_ge(high_ok, n + 1)
                        nc.vector.tensor_tensor(target(w, g, packs[w][2]), bank(w, g),
                                                target(w, g, packs[w][1]).bitcast(F32),
                                                ALU.subtract).then_inc(low_ok, 1)

                unpack(0)
                unpack(1)
                low_parts(0)
                unpack(2)
                low_parts(1)
                dve.wait_ge(x_seen, TILES)
                layernorm_factors(nc, dve, k, step, var_ok, std_ok)
                low_parts(2)

            @block.scalar
            def _(act):
                act.wait_ge(table_ok, 1)
                load_function_table(nc, k, ACT.Sqrt)
                def to_float(w):
                    act.wait_ge(odd_bits_ok, w + 1)
                    bits, _, out = scaled_groups(w, 1)
                    nc.scalar.activation(out, bits, ACT.Copy).then_inc(odd_float_ok, 1)

                def high_parts(w):
                    for g in range(HT):
                        act.wait_ge(turned_ok, w * HT + g + 1)
                        n = w * HT + g
                        nc.scalar.activation(target(w, g, packs[w][1]), bank(w, g), ACT.Copy).then_inc(high_ok, 1)
                        if n % 2 == 1:
                            if n // 2 >= 2:
                                act.wait_ge(odd_low_ok, n // 2 - 1)
                            nc.scalar.activation(whole_of(n, w, g), bank(w, g), ACT.Copy).then_inc(whole_ok, 1)

                to_float(0)
                to_float(1)
                high_parts(0)
                to_float(2)
                high_parts(1)
                act.wait_ge(var_ok, 1)
                nc.scalar.activation(k.std[:, :], k.var[:, :], ACT.Sqrt).then_inc(std_ok, 1)
                high_parts(2)

            @block.tensor
            def _(pe):
                pe.wait_ge(ident_ok, 1)
                for w in range(3):
                    pe.wait_ge(even_ok, w + 1)
                    pe.wait_ge(odd_ok, w + 1)
                    for g in range(HT):
                        n = w * HT + g
                        if n >= BANKS:
                            pe.wait_ge(whole_ok if n % 2 else low_ok, (n - BANKS) // 2 + 1)
                        blocks, rows, cols = source(w, g)
                        for b, blk in enumerate(blocks):
                            at = turned[n % BANKS][0:rows, b, 0:cols]
                            last = nc.tensor.transpose(at, blk, k.ident[0:blk.shape[0], 0:blk.shape[0]])
                        last.then_inc(turned_ok, 1)


def load_function_table(nc, k, function):
    nc.scalar.activation(k.table_out[:, :], k.table_in[:, :], function)


def layernorm_factors(nc, dve, k, step, var_ok, std_ok, tiles=range(TILES)):
    for t in tiles:
        last = nc.vector.bn_aggr(k.moments[:, t, :], k.stats[:, t, :])
    last.then_inc(step, 1)
    dve.wait_ge(step, 1)
    nc.vector.tensor_scalar(k.var[:, :], k.moments[:, :, 1], EPS, None, ALU.add).then_inc(var_ok, 1)
    nc.vector.tensor_copy(k.mean[:, :], k.moments[:, :, 0])
    dve.wait_ge(std_ok, 1)
    nc.vector.reciprocal(k.rstd[:, :], k.std[:, :]).then_inc(step, 1)
    dve.wait_ge(step, 2)


def ffn_phase(nc, k, src, dst, tag, stats):
    with ExitStack() as ctx:
        sb = lambda n, s, t: ctx.enter_context(nc.sbuf_tensor(tag + n, s, t))
        ps = lambda n, s: ctx.enter_context(nc.psum_tensor(tag + n, s, F32))
        sem = lambda n: ctx.enter_context(nc.semaphore(tag + n))
        xnh = sb("xnh", [P, KC, CHUNK], F32R)
        xnl = sb("xnl", [P, KC, CHUNK], F32R)
        gh = sb("gh", [P, HT, CHUNK], F32R)
        gl = sb("gl", [P, HT, CHUNK], F32R)
        xr = [sb(f"xr{i}", [P, C], F32) for i in range(2)]
        sa = [sb(f"sa{i}", [P, CHUNK], F32) for i in range(2)]
        g32 = [sb(f"g{i}", [P, CHUNK], F32) for i in range(2)]
        res = [sb(f"res{i}", [P, C], F32) for i in range(2)]
        pa = [ps(f"pa{i}", [P, CHUNK]) for i in range(2)]
        pb = [ps(f"pb{i}", [P, CHUNK]) for i in range(2)]
        pt = [ps(f"pt{i}", [P, KC, P]) for i in range(2)]
        py = [ps(f"py{i}", [P, C]) for i in range(2)]

        x_in = [sem(f"x_in{i}") for i in range(2)]
        xn_ok = sem("xn_ok")
        xt_ok = sem("xt_ok")
        xh_ok = sem("xh_ok")
        xl_ok = sem("xl_ok")
        ab_ok = sem("ab_ok")
        sa_ok = sem("sa_ok")
        g_ok = sem("g_ok")
        gh_ok = sem("gh_ok")
        gl_ok = sem("gl_ok")
        y_ok = sem("y_ok")
        r_in = [sem(f"r_in{i}") for i in range(2)]
        out_ok = sem("out_ok")
        stat_ok = sem("stat_ok")
        stored = [sem(f"stored{i}") for i in range(2)]
        step, var_ok, std_ok = sem("step"), sem("var_ok"), sem("std_ok")
        w2_moved = sem("w2_moved")

        def rows(n):
            return src[bass.ds((n & (TILES - 1)) * P, P), :] if not isinstance(n, int) else src[n * P:(n + 1) * P, :]

        with nc.Block() as block:
            @block.sync
            def _(sp):
                for t in range(2):
                    sp.dma_start(xr[t][:, :], rows(t)).then_inc(x_in[t], 16)
                for t in range(2):
                    sp.dma_start(res[t][:, :], rows(t + 2)).then_inc(r_in[t], 16)
                for t in range(2):
                    sp.wait_ge(xn_ok, t + 3)
                    sp.dma_start(res[t][:, :], rows(t)).then_inc(r_in[t], 16)

                def load_next(c, t):
                    wait_alone(sp, xt_ok, c * CT + CT + t - 1, x_in[0], 16)
                    sp.dma_start(xr[t % 2][:, :], rows(c * CT + CT + t)).then_inc(x_in[t % 2], 16)

                def store(c, t):
                    wait_alone(sp, stat_ok, c * CT + t + 1, x_in[0], 16)
                    sp.dma_start(dst[bass.ds((c * CT + t) * P, P), :], res[t % 2][:, :]).then_inc(stored[t % 2], 16)

                def load_residual(c, t):
                    wait_alone(sp, stored[t % 2], c * 32 + (t // 2 + 1) * 16, x_in[0], 16)
                    sp.dma_start(res[t % 2][:, :], rows(c * CT + t + 2)).then_inc(r_in[t % 2], 16)

                with sp.Fori(0, NCH) as c:
                    load_next(c, 0)
                    load_next(c, 1)
                    load_next(c, 2)
                    store(c, 0)
                    load_residual(c, 0)
                    load_next(c, 3)
                    for t in range(1, CT):
                        store(c, t)
                        load_residual(c, t)
                for i in range(2):
                    sp.wait_ge(stored[i], 16 * TILES // 2)
                    sp.wait_ge(r_in[i], 16 * (TILES // 2 + 2))
                    sp.wait_ge(x_in[i], 16 * (TILES + 2) // 2)

            @block.vector
            def _(dve):
                def normalise(n, t, k_in, source=xr, arrived=x_in):
                    dve.wait_ge(arrived[t % 2], k_in)
                    at = (n & (TILES - 1)) if not isinstance(n, int) else n
                    nc.vector.tensor_scalar(xr[t % 2][:, :], source[t % 2][:, :], k.mean[:, bass.ds(at, 1)],
                                            k.rstd[:, bass.ds(at, 1)], ALU.subtract, ALU.mult).then_inc(xn_ok, 1)

                def low_part(n, t):
                    dve.wait_ge(xh_ok, n + 1)
                    at = slice(t * P, (t + 1) * P)
                    nc.vector.tensor_tensor(xnl[:, :, at], pt[t % 2][:, :, :], xnh[:, :, at].bitcast(F32),
                                            ALU.subtract).then_inc(xl_ok, 1)

                for t in range(2):
                    normalise(t, t, 16)
                for t in range(CT):
                    low_part(t, t)
                    if t < 2:
                        normalise(t + 2, t, 16, res, r_in)

                with dve.Fori(0, NCH) as c:
                    for ht in range(HT):
                        n = hidden_rows(ht)
                        dve.wait_ge(sa_ok, c * HT + ht + 1)
                        if ht >= 2:
                            dve.wait_ge(gl_ok, c * HT + ht - 1)
                        nc.vector.tensor_tensor(g32[ht % 2][0:n, :], sa[ht % 2][0:n, :], pb[ht % 2][0:n, :],
                                                ALU.mult).then_inc(g_ok, 1)
                        if ht in (4, 6):
                            t = (ht - 4) // 2
                            normalise(c * CT + CT + t, t, c * 32 + 32)
                    for t in range(CT):
                        low_part(c * CT + CT + t, t)
                        if t < 2:
                            normalise(c * CT + CT + t + 2, t, c * 32 + 48)
                        dve.wait_ge(y_ok, c * CT + t + 1)
                        dve.wait_ge(r_in[t % 2], c * 32 + (t // 2 + 2) * 16)
                        nc.vector.scalar_tensor_tensor(out=res[t % 2][:, :], in0=py[t % 2][:, :], scalar=0.5,
                                                       in1=res[t % 2][:, :], op0=ALU.mult,
                                                       op1=ALU.add).then_inc(out_ok, 1)
                        dve.wait_ge(out_ok, c * CT + t + 1)
                        if stats:
                            nc.vector.bn_stats(k.stats[:, bass.ds(c * CT + t, 1), :].rearrange("p a s -> p (a s)"),
                                               res[t % 2][:, :]).then_inc(stat_ok, 1)
                        else:
                            dve.sem_inc(stat_ok, 1)
                if stats:
                    dve.wait_ge(stat_ok, TILES)
                    layernorm_factors(nc, dve, k, step, var_ok, std_ok)

            @block.scalar
            def _(act):
                def high_part(n, t):
                    act.wait_ge(xt_ok, n + 1)
                    if isinstance(n, int) and n >= 2:
                        act.wait_ge(xl_ok, n - 1)
                    nc.scalar.activation(xnh[:, :, t * P:(t + 1) * P], pt[t % 2][:, :, :], ACT.Copy).then_inc(xh_ok, 1)

                load_function_table(nc, k, ACT.Silu)
                for t in range(CT):
                    high_part(t, t)
                with act.Fori(0, NCH) as c:
                    for ht in range(HT):
                        n = hidden_rows(ht)
                        act.wait_ge(ab_ok, c * HT + ht + 1)
                        if ht >= 2:
                            act.wait_ge(g_ok, c * HT + ht - 1)
                        nc.scalar.activation(sa[ht % 2][0:n, :], pa[ht % 2][0:n, :], ACT.Silu).then_inc(sa_ok, 1)
                        act.wait_ge(g_ok, c * HT + ht + 1)
                        nc.scalar.activation(gh[0:n, ht, :], g32[ht % 2][0:n, :], ACT.Copy).then_inc(gh_ok, 1)
                    for t in range(CT):
                        high_part(c * CT + CT + t, t)
                if stats:
                    act.wait_ge(var_ok, 1)
                    nc.scalar.activation(k.std[:, :], k.var[:, :], ACT.Sqrt).then_inc(std_ok, 1)

            @block.gpsimd
            def _(pool):
                pool.wait_ge(xl_ok, CT)
                for part, far in zip((k.w2h, k.w2l), k.w2_parts):
                    for r, t in ((P, slice(0, HT - 1)), (HLAST, slice(HT - 1, HT))):
                        near, far_ = part[0:r, t, :].bitcast(F32), far[0:r, t, :]
                        to, from_ = (far_, near) if stats else (near, far_)
                        pool.dma_start(to, from_).then_inc(w2_moved, 16)
                with pool.Fori(0, NCH) as c:
                    for ht in range(HT):
                        n = hidden_rows(ht)
                        pool.wait_ge(gh_ok, c * HT + ht + 1)
                        nc.gpsimd.tensor_tensor(gl[0:n, ht, :], g32[ht % 2][0:n, :], gh[0:n, ht, :].bitcast(F32),
                                                ALU.subtract).then_inc(gl_ok, 1)
                pool.wait_ge(w2_moved, 64)

            @block.tensor
            def _(pe):
                def turn(n, t):
                    pe.wait_ge(xn_ok, n + 1)
                    if not isinstance(n, int) or n >= 2:
                        pe.wait_ge(xl_ok, n - 1)
                    for c4 in range(KC):
                        last = nc.tensor.transpose(pt[t % 2][:, c4, :], xr[t % 2][:, c4 * P:(c4 + 1) * P],
                                                   k.ident[:, :])
                    last.then_inc(xt_ok, 1)

                def product(out, wh, wl, ht):
                    n = hidden_rows(ht)
                    pairs = [(w[:, c4, ht * P:ht * P + n], x[:, c4, :])
                             for c4 in range(KC) for w, x in parts_of_product(wh, wl, xnh, xnl)]
                    for i, (w, x) in enumerate(pairs):
                        last = nc.tensor.matmul(out, w, x, start=i == 0, stop=i == len(pairs) - 1)
                    return last

                for t in range(CT):
                    turn(t, t)
                with pe.Fori(0, NCH) as c:
                    pe.wait_ge(xl_ok, c * CT + CT)
                    for ht in range(HT):
                        n = hidden_rows(ht)
                        if ht >= 2:
                            pe.wait_ge(g_ok, c * HT + ht - 1)
                        product(pa[ht % 2][0:n, :], k.w1h, k.w1l, ht)
                        product(pb[ht % 2][0:n, :], k.w3h, k.w3l, ht).then_inc(ab_ok, 1)
                    if not stats:
                        pe.wait_ge(w2_moved, 64)
                    for t in range(CT):
                        turn(c * CT + CT + t, t)
                        if t >= 2:
                            pe.wait_ge(out_ok, c * CT + t - 1)
                        for ht in range(HT):
                            n = hidden_rows(ht)
                            if t == 0:
                                pe.wait_ge(gl_ok, c * HT + ht + 1)
                            at = slice(t * P, (t + 1) * P)
                            for i, (g, w) in enumerate(parts_of_product(gh, gl, k.w2h, k.w2l)):
                                last = nc.tensor.matmul(py[t % 2][:, :], g[0:n, ht, at], w[0:n, ht, :],
                                                        start=ht == 0 and i == 0, stop=ht == HT - 1 and i == 2)
                        last.then_inc(y_ok, 1)


class WeightTurner:

    def __init__(self, nc, k, ctx, sources, parts, banks):
        sem = lambda n: ctx.enter_context(nc.semaphore("tq_" + n))
        self.nc, self.k, self.sources, self.parts, self.banks = nc, k, sources, parts, banks
        self.nat = [ctx.enter_context(nc.sbuf_tensor(f"tq_nat{i}", [P, KC, C], F32)) for i in range(2)]
        self.w_in = [sem(f"w_in{i}") for i in range(2)]
        self.turned = sem("turned")
        self.high = sem("high")
        self.low = sem("low")

    def load(self, sp, w):
        if w >= 2:
            sp.wait_ge(self.turned, KC * (w - 1))
        sp.dma_start(self.nat[w % 2][:, :, :], self.sources[w].rearrange("(o p) i -> p o i", p=P)
                     ).then_inc(self.w_in[w % 2], 16)

    def transpose(self, pe, w):
        pe.wait_ge(self.w_in[w % 2], 16 * (w // 2 + 1))
        for c4 in range(KC):
            n = w * KC + c4
            if n >= 4:
                pe.wait_ge(self.low, n - 3)
            for o in range(KC):
                last = self.nc.tensor.transpose(self.banks[n % 4][:, o * P:(o + 1) * P],
                                                self.nat[w % 2][:, o, c4 * P:(c4 + 1) * P], self.k.ident[:, :])
            last.then_inc(self.turned, 1)

    def high_parts(self, act, w):
        for n in range(w * KC, (w + 1) * KC):
            act.wait_ge(self.turned, n + 1)
            self.nc.scalar.activation(self.parts[w][0][:, n % KC, :], self.banks[n % 4], ACT.Copy).then_inc(self.high, 1)

    def low_parts(self, dve, w):
        for n in range(w * KC, (w + 1) * KC):
            dve.wait_ge(self.high, n + 1)
            self.nc.vector.tensor_tensor(self.parts[w][1][:, n % KC, :], self.banks[n % 4],
                                         self.parts[w][0][:, n % KC, :].bitcast(F32),
                                         ALU.subtract).then_inc(self.low, 1)


def qkv_phase(nc, d, k, src):
    with ExitStack() as ctx:
        sb = lambda n, s, t: ctx.enter_context(nc.sbuf_tensor(n, s, t))
        ps = lambda n, s: ctx.enter_context(nc.psum_tensor(n, s, F32))
        sem = lambda n: ctx.enter_context(nc.semaphore("q_" + n))
        parts = [(sb(f"{w}h", [P, KC, C], F32R), sb(f"{w}l", [P, KC, C], F32R)) for w in ("wq", "wk", "wv")]
        xr = [sb(f"qxr{i}", [P, C], F32) for i in range(2)]
        xh = [sb(f"qxh{i}", [P, KC, P], F32R) for i in range(2)]
        xl = [sb(f"qxl{i}", [P, KC, P], F32R) for i in range(2)]
        turn = [sb(f"turn{i}", [P, 3], F32) for i in range(2)]
        by_cos = sb("by_cos", [P, C], F32)
        roped = [sb(f"roped{i}", [P, C], F32) for i in range(2)]
        th = [sb(f"th{i}", [P, KC, P], F32R) for i in range(2)]
        tl = [sb(f"tl{i}", [P, KC, P], F32R) for i in range(2)]
        va = sb("va", [P, H, ONES], F32)
        pt = ps("q_pt", [P, KC, P])
        pj = [ps(f"q_pj{i}", [P, C]) for i in range(3)]
        pr = [ps(f"q_pr{i}", [P, KC, P]) for i in range(2)]
        weights = WeightTurner(nc, k, ctx, [d["wq"], d["wk"], d["wv"], d["wo"]], parts + [(k.woh, k.wol)],
                               [bank[:, :] for bank in pj] + [pr[0][:, :, :].rearrange("p c t -> p (c t)")])

        x_in = [sem(f"x_in{i}") for i in range(2)]
        xn_ok, xt_ok, xh_ok, xl_ok = sem("xn_ok"), sem("xt_ok"), sem("xh_ok"), sem("xl_ok")
        pj_ok = [sem(f"pj_ok{i}") for i in range(3)]
        cos_ok = [sem(f"cos_ok{i}") for i in range(2)]
        rope_ok = [sem(f"rope_ok{i}") for i in range(2)]
        v_ok = sem("v_ok")
        rt_ok = [sem(f"rt_ok{i}") for i in range(2)]
        th_ok = [sem(f"th_ok{i}") for i in range(2)]
        tl_ok = [sem(f"tl_ok{i}") for i in range(2)]
        th_out = [sem(f"th_out{i}") for i in range(2)]
        tl_out = [sem(f"tl_out{i}") for i in range(2)]
        v_out = sem("v_out")
        ones_ok = sem("ones_ok")

        def rows(n):
            return src[bass.ds((n & (TILES - 1)) * P, P), :] if not isinstance(n, int) else src[n * P:(n + 1) * P, :]

        with nc.Block() as block:
            @block.sync
            def _(sp):
                for w in range(2):
                    weights.load(sp, w)
                for t in range(2):
                    sp.dma_start(xr[t][:, :], rows(t)).then_inc(x_in[t], 16)
                for w in range(2, 4):
                    weights.load(sp, w)
                for b in range(B):
                    with sp.Fori(0, QT // 2) as j:
                        i = j + b * (QT // 2)
                        for s in range(2):
                            wait_alone(sp, xt_ok, 2 * i + s + 1, x_in[0], 16)
                            sp.dma_start(xr[s][:, :], rows(2 * i + s + 2)).then_inc(x_in[s], 16)
                            toks = bass.ds((2 * j + s) * P, P)
                            rowsb = slice(b * C, (b + 1) * C)
                            for m, (hi, lo) in enumerate(((k.qh, k.ql), (k.kh, k.kl))):
                                wait_alone(sp, th_ok[m], 2 * i + s + 1, x_in[0], 16)
                                sp.dma_start(hi[rowsb, toks].rearrange("(g p) q -> p g q", p=P),
                                             th[m][:, :, :].bitcast(F32)).then_inc(th_out[m], 16)
                                wait_alone(sp, tl_ok[m], 2 * i + s + 1, x_in[0], 16)
                                sp.dma_start(lo[rowsb, toks].rearrange("(g p) q -> p g q", p=P),
                                             tl[m][:, :, :].bitcast(F32)).then_inc(tl_out[m], 16)
                            wait_alone(sp, v_ok, 2 * i + s + 1, x_in[0], 16)
                            sp.dma_start(k.v[b * (H // 4):(b + 1) * (H // 4), toks, :].rearrange("a q c -> q a c"),
                                         va[:, :, :].rearrange("p (a h) c -> p a (h c)", h=4)).then_inc(v_out, 16)
                for m in range(2):
                    sp.wait_ge(th_out[m], 16 * TILES)
                    sp.wait_ge(tl_out[m], 16 * TILES)
                    sp.wait_ge(x_in[m], 16 * (TILES // 2 + 1))
                sp.wait_ge(v_out, 16 * TILES)

            @block.gpsimd
            def _(pool):
                pool.memset(va[:, :, :], 1.0).then_inc(ones_ok, 1)

            @block.vector
            def _(dve):
                def normalise(n, s, count):
                    dve.wait_ge(x_in[s], count)
                    at = (n & (TILES - 1)) if not isinstance(n, int) else n
                    nc.vector.tensor_scalar(xr[s][:, :], xr[s][:, :], k.mean[:, bass.ds(at, 1)],
                                            k.rstd[:, bass.ds(at, 1)], ALU.subtract, ALU.mult).then_inc(xn_ok, 1)

                def low_x(n, s):
                    dve.wait_ge(xh_ok, n + 1)
                    nc.vector.tensor_tensor(xl[s][:, :, :], pt[:, :, :], xh[s][:, :, :].bitcast(F32),
                                            ALU.subtract).then_inc(xl_ok, 1)

                def angles(n, s):
                    at = (n & (QT - 1)) if not isinstance(n, int) else n
                    nc.vector.tensor_copy(turn[s][:, :].unsqueeze(2), k.rope[:, :, bass.ds(at, 1)])

                def rotate(n, s, m):
                    dve.wait_ge(cos_ok[m], n + 1)
                    pairs = lambda a: a[:, :].rearrange("p (h two) -> p h two", two=2)
                    x, c, o = pairs(pj[m]), pairs(by_cos), pairs(roped[m])
                    nc.vector.scalar_tensor_tensor(out=o[:, :, 0], in0=x[:, :, 1], scalar=turn[s][:, 2:3],
                                                   in1=c[:, :, 0], op0=ALU.mult, op1=ALU.add)
                    nc.vector.scalar_tensor_tensor(out=o[:, :, 1], in0=x[:, :, 0], scalar=turn[s][:, 1:2],
                                                   in1=c[:, :, 1], op0=ALU.mult, op1=ALU.add).then_inc(rope_ok[m], 1)

                def low_t(n, m, first):
                    dve.wait_ge(th_ok[m], n + 1)
                    if not first:
                        dve.wait_ge(tl_out[m], 16 * n)
                    nc.vector.tensor_tensor(tl[m][:, :, :], pr[m][:, :, :], th[m][:, :, :].bitcast(F32),
                                            ALU.subtract).then_inc(tl_ok[m], 1)

                def tile(n, s, count, first=False):
                    rotate(n, s, 0)
                    low_x(n + 1, 1 - s)
                    rotate(n, s, 1)
                    normalise(n + 2, s, count)
                    dve.wait_ge(rope_ok[1], n + 1)
                    angles(n + 2, s)
                    low_t(n, 0, first)
                    low_t(n, 1, first)

                angles(0, 0)
                angles(1, 1)
                weights.low_parts(dve, 0)
                normalise(0, 0, 16)
                normalise(1, 1, 16)
                weights.low_parts(dve, 1)
                weights.low_parts(dve, 2)
                low_x(0, 0)
                weights.low_parts(dve, 3)
                tile(0, 0, 32, True)
                tile(1, 1, 32)
                with dve.Fori(1, TILES // 2) as i:
                    for s in range(2):
                        tile(2 * i + s, s, i * 16 + 32)

            @block.scalar
            def _(act):
                def high_x(n, s):
                    act.wait_ge(xt_ok, n + 1)
                    nc.scalar.activation(xh[s][:, :, :], pt[:, :, :], ACT.Copy).then_inc(xh_ok, 1)

                def cos_part(n, s, m, first):
                    act.wait_ge(pj_ok[m], n + 1)
                    if m == 1:
                        act.wait_ge(rope_ok[0], n + 1)
                    elif not first:
                        act.wait_ge(rope_ok[1], n)
                    nc.scalar.activation(by_cos[:, :], pj[m][:, :], ACT.Copy,
                                         scale=turn[s][:, 0:1]).then_inc(cos_ok[m], 1)

                def tile(n, s, first=False):
                    cos_part(n, s, 0, first)
                    high_x(n + 1, 1 - s)
                    cos_part(n, s, 1, first)
                    act.wait_ge(pj_ok[2], n + 1)
                    if not first:
                        act.wait_ge(v_out, 16 * n)
                    nc.scalar.activation(va[:, :, 0:D], pj[2][:, :].rearrange("p (h c) -> p h c", c=D),
                                         ACT.Copy).then_inc(v_ok, 1)
                    for m in range(2):
                        act.wait_ge(rt_ok[m], n + 1)
                        if not first:
                            act.wait_ge(th_out[m], 16 * n)
                        nc.scalar.activation(th[m][:, :, :], pr[m][:, :, :], ACT.Copy).then_inc(th_ok[m], 1)

                for w in range(3):
                    weights.high_parts(act, w)
                high_x(0, 0)
                weights.high_parts(act, 3)
                act.wait_ge(ones_ok, 1)
                tile(0, 0, True)
                tile(1, 1)
                with act.Fori(1, TILES // 2) as i:
                    for s in range(2):
                        tile(2 * i + s, s)

            @block.tensor
            def _(pe):
                def turn_x(n, s):
                    pe.wait_ge(xn_ok, n + 1)
                    for c4 in range(KC):
                        last = nc.tensor.transpose(pt[:, c4, :], xr[s][:, c4 * P:(c4 + 1) * P], k.ident[:, :])
                    last.then_inc(xt_ok, 1)

                def project(m, s):
                    pairs = [(x[:, c4, :], w[:, c4, :]) for c4 in range(KC)
                             for x, w in parts_of_product(xh[s], xl[s], *parts[m])]
                    for i, (x, w) in enumerate(pairs):
                        last = nc.tensor.matmul(pj[m][:, :], x, w, start=i == 0, stop=i == len(pairs) - 1)
                    last.then_inc(pj_ok[m], 1)

                def tile(n, s, first=False):
                    pe.wait_ge(xl_ok, n + 1)
                    if not first:
                        pe.wait_ge(rope_ok[0], n)
                    project(0, s)
                    turn_x(n + 1, 1 - s)
                    if not first:
                        pe.wait_ge(rope_ok[1], n)
                    project(1, s)
                    if not first:
                        pe.wait_ge(v_ok, n)
                    project(2, s)
                    for m in range(2):
                        pe.wait_ge(rope_ok[m], n + 1)
                        if not first:
                            pe.wait_ge(tl_ok[m], n)
                        for c4 in range(KC):
                            last = nc.tensor.transpose(pr[m][:, c4, :], roped[m][:, c4 * P:(c4 + 1) * P],
                                                       k.ident[:, :])
                        last.then_inc(rt_ok[m], 1)

                for w in range(3):
                    weights.transpose(pe, w)
                turn_x(0, 0)
                weights.transpose(pe, 3)
                pe.wait_ge(weights.low, 4 * KC)
                tile(0, 0, True)
                tile(1, 1)
                with pe.Fori(1, TILES // 2) as i:
                    for s in range(2):
                        tile(2 * i + s, s)



HQ = QT // 2
PARTS = 4
MROW = P - 2


def score_units():
    units = [(1,)]
    for i in range(QT):
        for half in range(i // HQ + 1):
            width = min(HALF, (i + 1) * P - half * HALF)
            together = HALF // width
            for h in range(0, 4, together):
                units.append((i, half, range(h, min(h + together, 4)), width))
    first = 1 + sum(1 for u in units[1:] if u[0] < HQ)
    units.insert(first + 3, (0,))
    return units


def attention_steps():
    return [(half, j, max(half * HALF, j * P)) for half in range(2) for j in range(HQ * (half + 1))]


def attention_phase(nc, k):
    UNITS, STEPS = score_units(), attention_steps()
    NU, NS = len(UNITS), len(STEPS)
    A_UNITS = 1 + sum(1 for u in UNITS if len(u) > 1 and u[0] < HQ)
    BATCH = 1
    AHEAD = 1
    RING = 2
    FIXED = 1000
    assert RING >= AHEAD + BATCH and NS % RING == 0 and HQ % BATCH == 0
    LOADS = 2 * PARTS
    with ExitStack() as ctx:
        sb = lambda n, s, t: ctx.enter_context(nc.sbuf_tensor("a_" + n, s, t))
        ps = lambda n, s: ctx.enter_context(nc.psum_tensor("a_" + n, s, F32))
        sem = lambda n: ctx.enter_context(nc.semaphore("a_" + n))
        qs = [sb(f"qs{i}", [P, 2, 4, HALF], F32R) for i in range(2)]
        ks = [sb(f"ks{i}", [P, 2, 4, HALF], F32R) for i in range(2)]
        vq = [sb(f"vq{i}", [P, QT, 4, ONES], F32) for i in range(2)]
        pr = [sb(f"probs{i}", [P, 4, HALF], F32) for i in range(RING)]
        osb = [sb(f"osb{i}", [P, HALF], F32) for i in range(2)]
        mx = [sb(f"rowmax{i}", [P, P], F32) for i in range(2)]
        by_half = [sb(f"max_half{i}", [P, 4 * HQ], F32) for i in range(2)]
        mh = [sb(f"mh{i}", [4 * HQ, P], F32R) for i in range(2)]
        ml = [sb(f"ml{i}", [4 * HQ, P], F32R) for i in range(2)]
        mask = sb("mask", [P, P], BF16)
        mask_t = sb("mask_t", [P, P], BF16)
        identb = sb("identb", [P, P], BF16)
        psc = [ps(f"psc{i}", [P, HALF]) for i in range(3)]
        pst = [ps(f"pst{i}", [P, 2, HALF]) for i in range(2)]
        po = ps("po", [P, HALF])

        const_z, const_ok = sem("const_z"), sem("const_ok")
        clear_ok, clear2_ok = sem("clear_ok"), sem("clear2_ok")
        qk_in = [[sem(f"qk_in{i}{half}") for half in range(2)] for i in range(2)]
        v_in = [sem(f"v_in{i}") for i in range(2)]
        sc_ok = sem("sc_ok")
        mx_ok = sem("mx_ok")
        mxb_ok = sem("mxb_ok")
        mstep = sem("mstep")
        m_in = [sem(f"m_in{i}") for i in range(2)]
        st_ok = sem("st_ok")
        ex_ok = sem("ex_ok")
        pv_ok = sem("pv_ok")
        o_ok = sem("o_ok")
        o_out = [sem(f"o_out{i}") for i in range(2)]
        sums = sb("sums", [2 * H, HALF], F32)
        sums_in, inverted, inv_out = sem("sums_in"), sem("inverted"), sem("inv_out")
        osb_ok = sem("osb_ok")

        def quads(eng):
            with eng.Fori(0, QUADS // 2 - 1) as it:
                yield 2 * it, 0
                yield 2 * it + 1, 1
            yield QUADS - 2, 0
            yield QUADS - 1, 1

        def more(q, ahead):
            return not isinstance(q, int) or q + ahead < QUADS

        def loaded(q, s, dmas):
            return (q - s) * (8 * dmas) + 16 * dmas

        def two_heads(pair, width):
            flat = pst[pair][:, :, :].rearrange("p x w -> p (x w)")
            step = width if 2 * width <= HALF else HALF
            return flat[:, 0:2 * step].rearrange("p (x w) -> p x w", w=step)[:, :, 0:width]

        weights = [(half + 1) * HALF - q0 + FIXED for half, j, q0 in (STEPS[AHEAD:] + STEPS[:AHEAD]) for _ in range(2)]
        issued = [0] + [round(NU * sum(weights[1:i + 1]) / sum(weights[1:])) for i in range(1, 2 * NS)]

        with nc.Block() as block:
            @block.sync
            def _(sp):
                def load(q, s, half):
                    at = slice(half * HALF, (half + 1) * HALF)
                    for stack, scratches in ((qs[s], (k.qh, k.qh, k.ql, k.ql)), (ks[s], (k.kh, k.kl, k.kh, k.kl))):
                        for part, scratch in enumerate(scratches):
                            src = scratch[bass.ds(q * (4 * D), 4 * D), at].rearrange("(h d) t -> d h t", d=D)
                            sp.dma_start(stack[part * D:(part + 1) * D, half, :, :].bitcast(F32), src
                                         ).then_inc(qk_in[s][half], 16)

                def put_max(q, s, half):
                    sp.wait_ge(mx_ok, (q + half) * NU + UNITS.index((half,)) + 1)
                    for x, m in enumerate((mh[half], ml[half])):
                        sp.dma_start(qs[s][MROW + x:MROW + x + 1, half, :, :].rearrange("o h t -> o (h t)").bitcast(F32),
                                     m[:, :].bitcast(F32)).then_inc(m_in[half], 16)

                for half in range(2):
                    load(0, 0, half)
                for half in range(2):
                    load(1, 1, half)
                sp.wait_ge(clear_ok, 2)
                sp.wait_ge(clear2_ok, 4)
                put_max(0, 0, 0)
                for q, s in quads(sp):
                    if not more(q, 2) and s == 0:
                        for half in range(2):
                            sp.wait_ge(o_out[half], 16 * (QUADS // 2 + 1))
                        move_sums(sp, k, sums, 0, True, sums_in)
                    put_max(q, s, 1)
                    if more(q, 1):
                        put_max(q + 1, 1 - s, 0)
                    if more(q, 2):
                        wait_alone(sp, pv_ok, q * NS + 2 * HQ, qk_in[0][0], 16)
                        load(q + 2, s, 0)
                        wait_alone(sp, pv_ok, q * NS + NS, qk_in[0][0], 16)
                        load(q + 2, s, 1)
                sp.wait_ge(inverted, 1)
                move_sums(sp, k, sums, 0, False, inv_out)
                sp.wait_ge(inv_out, 32)
                for i in range(2):
                    sp.wait_ge(m_in[i], 32 * QUADS)

            @block.gpsimd
            def _(pool):
                def load_v(q, s):
                    pool.dma_start(vq[s][:, :, :, :].rearrange("p j h c -> p j (h c)"),
                                   k.v[bass.ds(q, 1), :, :].rearrange("o (j p) c -> p (o j) c", p=P)
                                   ).then_inc(v_in[s], 16)

                pool.memset(mask[:, :], 0.0).then_inc(const_z, 1)
                pool.memset(mask_t[:, :], 0.0).then_inc(const_z, 1)
                pool.memset(identb[:, :], 0.0).then_inc(const_z, 1)
                pool.wait_ge(const_z, 3)
                pool.affine_select(out=mask[:, :], in_=mask[:, :], compare_op=ALU.is_ge, fill=NEG, base=0,
                                   pattern=[[-1, P]], channel_multiplier=1).then_inc(const_ok, 1)
                pool.affine_select(out=mask_t[:, :], in_=mask_t[:, :], compare_op=ALU.is_ge, fill=NEG, base=0,
                                   pattern=[[1, P]], channel_multiplier=-1).then_inc(const_ok, 1)
                pool.affine_select(out=identb[:, :], in_=identb[:, :], compare_op=ALU.not_equal, fill=1.0,
                                   base=0, pattern=[[-1, P]], channel_multiplier=1).then_inc(const_ok, 1)
                pool.wait_ge(const_ok, 3)
                pool.memset(qs[0][PARTS * D:P, 1, :, :].bitcast(F32), 0.0).then_inc(clear2_ok, 1)
                pool.memset(ks[0][PARTS * D:P, 1, :, :].bitcast(F32), 1.0).then_inc(clear2_ok, 1)
                pool.memset(qs[1][PARTS * D:P, :, :, :].bitcast(F32), 0.0).then_inc(clear2_ok, 1)
                pool.memset(ks[1][PARTS * D:P, :, :, :].bitcast(F32), 1.0).then_inc(clear2_ok, 1)
                for s in range(2):
                    load_v(s, s)
                pool.wait_ge(clear2_ok, 4)
                for i in range(2):
                    pool.memset(osb[i][:, :], 0.0).then_inc(osb_ok, 1)
                pool.wait_ge(osb_ok, 2)
                for half in range(2):
                    pool.dma_start(k.o[0:P, half * HALF:(half + 1) * HALF], osb[half][:, :]).then_inc(o_out[half], 16)
                for q, s in quads(pool):
                    for half in range(2):
                        wait_alone(pool, o_ok, 2 * q + half + 2, const_ok, 3)
                        pool.dma_start(k.o[bass.ds(q * P, P), half * HALF:(half + 1) * HALF],
                                       osb[half][:, :]).then_inc(o_out[half], 16)
                    if more(q, 2):
                        load_v(q + 2, s)
                for i in range(2):
                    pool.wait_ge(o_out[i], 16 * (QUADS + 1))

            @block.vector
            def _(dve):
                def unit(u, q):
                    if len(UNITS[u]) == 1:
                        return split(u, q, UNITS[u][0])
                    i, half, heads, width = UNITS[u]
                    dve.wait_ge(sc_ok, q * NU + u + 1)
                    nh = len(heads)
                    to = mx[0][:, 0:4 * HQ] if i < HQ else by_half[half][:, :]
                    to = to.rearrange("p (h i) -> p h i", h=4)[:, heads[0]:heads[0] + nh, i % HQ]
                    nc.vector.tensor_reduce(to, psc[u % 3][:, 0:nh * width].rearrange("p (h w) -> p h w", h=nh),
                                            AX.X, ALU.max).then_inc(mx_ok, 1)
                    if u == NU - 1:
                        dve.wait_ge(mx_ok, q * NU + u + 1)
                        nc.vector.tensor_tensor(mx[1][:, 0:4 * HQ], by_half[0][:, :], by_half[1][:, :],
                                                ALU.max).then_inc(mxb_ok, 1)

                def split(u, q, half):
                    dve.wait_ge(sc_ok, q * NU + u + 1)
                    turned = psc[u % 3][0:4 * HQ, 0:P]
                    nc.vector.tensor_scalar(mh[half][:, :], turned, -1.0, None, ALU.mult).then_inc(mstep, 1)
                    dve.wait_ge(mstep, q * 2 + (1 - half) + 1 + clears)
                    nc.vector.scalar_tensor_tensor(out=ml[half][:, :], in0=turned, scalar=-1.0,
                                                   in1=mh[half][:, :].bitcast(F32), op0=ALU.mult,
                                                   op1=ALU.subtract).then_inc(mx_ok, 1)

                clears = 2
                for i in range(2):
                    nc.vector.memset(mx[i][:, :], 0.0).then_inc(mstep, 1)
                nc.vector.memset(qs[0][PARTS * D:P, 0, :, :].bitcast(F32), 0.0).then_inc(clear_ok, 1)
                nc.vector.memset(ks[0][PARTS * D:P, 0, :, :].bitcast(F32), 1.0).then_inc(clear_ok, 1)
                nc.vector.memset(po[:, :], 0.0).then_inc(o_ok, 1)
                dve.wait_ge(mstep, clears)
                for u in range(NU):
                    unit(u, 0)
                for q, s in quads(dve):
                    if more(q, 1):
                        for u in range(NU):
                            unit(u, q + 1)
                    else:
                        unit(0, q + 1)
                dve.wait_ge(sums_in, 32)
                nc.vector.reciprocal(sums[:, :], sums[:, :]).then_inc(inverted, 1)

            @block.scalar
            def _(act):
                def exps(n, q):
                    half, j, q0 = STEPS[n]
                    width = (half + 1) * HALF - q0
                    for pair in range(2):
                        act.wait_ge(st_ok, q * (2 * NS) + 2 * n + pair + 1)
                        nc.scalar.activation(pr[n % RING][:, 2 * pair:2 * pair + 2, 0:width],
                                             two_heads(pair, width), ACT.Exp, scale=SCALE).then_inc(ex_ok, 1)

                def output(half, q):
                    act.wait_ge(pv_ok, q * NS + (HQ if half == 0 else NS))
                    act.wait_ge(o_out[half], q * 16 + 16)
                    nc.scalar.activation(osb[half][:, :], po[:, :], ACT.Copy).then_inc(o_ok, 1)

                for n in range(AHEAD):
                    exps(n, 0)
                for q, s in quads(act):
                    for n in range(AHEAD, NS):
                        exps(n, q)
                        if n == HQ + AHEAD - 1:
                            output(0, q)
                    if more(q, 1):
                        for n in range(AHEAD):
                            exps(n, q + 1)
                    output(1, q)

            @block.tensor
            def _(pe):
                def add_mask(tiles, m):
                    return nc.tensor.matmul(tiles, identb[:, :], m[:, :].unsqueeze(1).broadcast_to(tiles.shape),
                                            start=False, stop=True)

                def unit(u, q, s):
                    before = u - 3 if u >= 3 else max(v for v in range(NU) if v % 3 == u) - NU
                    if before >= 0 or not isinstance(q, int) or q > 0:
                        pe.wait_ge(mx_ok, q * NU + before + 1)
                    if len(UNITS[u]) == 1:
                        if UNITS[u][0] == 1 and (not isinstance(q, int) or q > 0):
                            pe.wait_ge(mxb_ok, q)
                        nc.tensor.transpose(psc[u % 3][:, 0:P], mx[UNITS[u][0]][:, :], k.ident[:, :]
                                            ).then_inc(sc_ok, 1)
                        return
                    i, half, heads, width = UNITS[u]
                    if u == 1:
                        pe.wait_ge(qk_in[s][0], loaded(q, s, LOADS))
                    if u == A_UNITS:
                        pe.wait_ge(qk_in[s][1], loaded(q, s, LOADS))
                    diagonal = (i + 1) * P == half * HALF + width
                    out = psc[u % 3][:, 0:len(heads) * width].rearrange("p (h w) -> p h w", w=width)
                    for x, h in enumerate(heads):
                        last = nc.tensor.matmul(out[:, x, :], qs[s][0:MROW, i // HQ, h, bass.ts(i % HQ, P)],
                                                ks[s][0:MROW, half, h, 0:width],
                                                start=x == 0, stop=h == heads[-1] and not diagonal)
                    if diagonal:
                        last = add_mask(out[:, :, width - P:width], mask)
                    last.then_inc(sc_ok, 1)

                def scores(n, q, s, pair):
                    half, j, q0 = STEPS[n]
                    width = (half + 1) * HALF - q0
                    if j == 0 and pair == 0:
                        pe.wait_ge(m_in[half], q * 32 + 32)
                    if n > 0 or not isinstance(q, int) or q > 0:
                        pe.wait_ge(ex_ok, q * (2 * NS) + 2 * n - 1 + pair)
                    out, diagonal = two_heads(pair, width), q0 == j * P
                    shared = 2 * width <= HALF
                    for x in range(2):
                        h = 2 * pair + x
                        last = nc.tensor.matmul(out[:, x, :], ks[s][0:P, j // HQ, h, bass.ts(j % HQ, P)],
                                                qs[s][0:P, half, h, HALF - width:HALF],
                                                start=x == 0 or not shared,
                                                stop=not diagonal and (x == 1 or not shared))
                    if diagonal:
                        for x in ([slice(0, 2)] if shared else [slice(0, 1), slice(1, 2)]):
                            last = add_mask(out[:, x, 0:P], mask_t)
                    last.then_inc(st_ok, 1)

                def values(n, q, s):
                    half, j, q0 = STEPS[n]
                    width = (half + 1) * HALF - q0
                    pe.wait_ge(ex_ok, q * (2 * NS) + 2 * n + 2)
                    if n == 0:
                        pe.wait_ge(v_in[s], loaded(q, s, 1))
                    if j == 0:
                        pe.wait_ge(o_ok, 2 * q + half + 1)
                    for h in range(4):
                        last = nc.tensor.matmul(po[32 * h:32 * h + ONES, q0 - half * HALF:HALF],
                                                vq[s][:, j, h, :], pr[n % RING][:, h, 0:width],
                                                start=j == 0, stop=j == HQ * (half + 1) - 1,
                                                tile_position=(0, 32 * h))
                    last.then_inc(pv_ok, 1)

                def quad(q, s):
                    done = 0
                    for n0 in range(0, NS, BATCH):
                        for x in range(2 * BATCH):
                            n, pair = n0 + AHEAD + x // 2, x % 2
                            if n < NS:
                                scores(n, q, s, pair)
                            elif more(q, 1):
                                scores(n - NS, q + 1, 1 - s, pair)
                            upto = issued[2 * n0 + x]
                            for u in range(done, upto):
                                if more(q, 1) or u == 0:
                                    unit(u, q + 1, 1 - s)
                            done = upto
                        for n in range(n0, n0 + BATCH):
                            values(n, q, s)

                pe.wait_ge(const_ok, 3)
                pe.wait_ge(mstep, 2)
                pe.wait_ge(clear_ok, 2)
                for u in range(NU):
                    if u == A_UNITS:
                        pe.wait_ge(clear2_ok, 2)
                    unit(u, 0, 0)
                for n in range(AHEAD):
                    for pair in range(2):
                        scores(n, 0, 0, pair)
                pe.wait_ge(clear2_ok, 4)
                for q, s in quads(pe):
                    quad(q, s)


def move_sums(sp, k, sums, b, load, done):
    rows = slice(b * (H // 4), (b + 1) * (H // 4))
    for x in range(2):
        at = slice(x * HALF, (x + 1) * HALF)
        on_chip = sums[x * H:(x + 1) * H, :]
        if load:
            o4 = k.o.rearrange("(q h r) t -> q h r t", h=4, r=32)
            sp.dma_start(on_chip, o4[rows, :, D, at].rearrange("q h t -> (q h) t")).then_inc(done, 16)
        else:
            sp.dma_start(k.inverse[rows, :, at].rearrange("q h t -> (q h) t"), on_chip).then_inc(done, 16)


def project_phase(nc, d, k, src, dst):
    with ExitStack() as ctx:
        sb = lambda n, s, t: ctx.enter_context(nc.sbuf_tensor("o_" + n, s, t))
        ps = lambda n, s: ctx.enter_context(nc.psum_tensor("o_" + n, s, F32))
        sem = lambda n: ctx.enter_context(nc.semaphore("o_" + n))
        W = 2 * P
        NB = TOK // W
        L = 2 * W
        NL = T // L
        sums = sb("sums", [2 * H, HALF], F32)
        on = [sb(f"on{i}", [P, KC, L], F32) for i in range(2)]
        sm = [sb(f"sm{i}", [P, KC, L], F32) for i in range(2)]
        oh = [sb(f"oh{i}", [P, KC, W], F32R) for i in range(2)]
        ol = [sb(f"ol{i}", [P, KC, W], F32R) for i in range(2)]
        R = 4
        res = sb("res", [P, TILES, C], F32)
        py = [ps(f"py{i}", [P, C]) for i in range(4)]
        sums_in, inverted, inv_out = sem("sums_in"), sem("inverted"), sem("inv_out")
        o_in = [sem(f"o_in{i}") for i in range(2)]
        norm_ok, oh_ok, ol_ok = sem("norm_ok"), sem("oh_ok"), sem("ol_ok")
        y_ok, out_ok, stat_ok = sem("y_ok"), sem("out_ok"), sem("stat_ok")
        r_in = [sem(f"r_in{i}") for i in range(TILES // R)]
        stored = sem("stored")
        step, var_ok, std_ok = sem("step"), sem("var_ok"), sem("std_ok")
        o4 = k.o.rearrange("(q h r) t -> q h r t", h=4, r=32)
        with nc.Block() as block:
            @block.sync
            def _(sp):
                for n in range(B * NL):
                    b, at = n // NL, slice(n % NL * L, (n % NL + 1) * L)
                    s = n % 2
                    if n == NL:
                        sp.wait_ge(inverted, 1)
                        move_sums(sp, k, sums, 1, False, inv_out)
                        sp.wait_ge(inv_out, 32)
                    if n >= 2:
                        sp.wait_ge(ol_ok, 2 * (n - 1))
                    for g in range(KC):
                        q = b * (H // 4) + 2 * g
                        sp.dma_start(on[s][:, g, :], o4[q:q + 2, :, 0:D, at].rearrange("q h r t -> (q h) r t")
                                     ).then_inc(o_in[s], 16)
                        sp.dma_start(sm[s][:, g, :], k.inverse[q:q + 2, :, at].rearrange("q h t -> (q h) t")
                                     .unsqueeze(1).broadcast_to([8, D, L])).then_inc(o_in[s], 16)
                    if n == 0:
                        move_sums(sp, k, sums, 1, True, sums_in)

            @block.gpsimd
            def _(pool):
                for n in range(NB):
                    if n % 2 == 0:
                        pool.wait_ge(o_in[n // 2 % 2], 16 * 2 * KC * (n // 4 + 1))
                    s, at = n // 2 % 2, slice(n % 2 * W, (n % 2 + 1) * W)
                    nc.gpsimd.tensor_tensor(on[s][:, :, at], on[s][:, :, at], sm[s][:, :, at], ALU.mult).then_inc(norm_ok, 1)

            @block.vector
            def _(dve):
                def low_part(n):
                    dve.wait_ge(oh_ok, n + 1)
                    nc.vector.tensor_tensor(ol[n % 2][:, :, :], on[n // 2 % 2][:, :, n % 2 * W:(n % 2 + 1) * W],
                                            oh[n % 2][:, :, :].bitcast(F32), ALU.subtract).then_inc(ol_ok, 1)

                low_part(0)
                dve.wait_ge(sums_in, 32)
                nc.vector.reciprocal(sums[:, :], sums[:, :]).then_inc(inverted, 1)
                low_part(1)
                for n in range(NB):
                    for t in range(2):
                        m = 2 * n + t
                        dve.wait_ge(y_ok, m + 1)
                        dve.wait_ge(r_in[m // R], 16)
                        nc.vector.tensor_tensor(res[:, m, :], res[:, m, :], py[m % 4][:, :],
                                                ALU.add).then_inc(out_ok, 1)
                        if t == 1 and n + 2 < NB:
                            low_part(n + 2)
                        dve.wait_ge(out_ok, m + 1)
                        nc.vector.bn_stats(k.stats[:, m, :], res[:, m, :]).then_inc(stat_ok, 1)
                        if m > 0:
                            dve.wait_ge(stat_ok, m)
                            nc.vector.bn_aggr(k.moments[:, m - 1, :], k.stats[:, m - 1, :])
                dve.wait_ge(stat_ok, TILES)
                layernorm_factors(nc, dve, k, step, var_ok, std_ok, [TILES - 1])

            @block.scalar
            def _(act):
                load_function_table(nc, k, ACT.Sqrt)

                def rows(x, m, n):
                    return x[m * P:(m + n) * P, :].rearrange("(t p) c -> p t c", p=P)

                def load_residual(i):
                    act.dma_start(res[:, R * i:R * (i + 1), :], rows(src, R * i, R)).then_inc(r_in[i], 16)

                def high_part(n):
                    act.wait_ge(norm_ok, n + 1)
                    if n >= 2:
                        act.wait_ge(y_ok, 2 * (n - 1))
                    nc.scalar.activation(oh[n % 2][:, :, :], on[n // 2 % 2][:, :, n % 2 * W:(n % 2 + 1) * W],
                                         ACT.Copy).then_inc(oh_ok, 1)

                high_part(0)
                load_residual(0)
                high_part(1)
                for n in range(NB):
                    if n + 2 < NB:
                        high_part(n + 2)
                    if n + 1 < TILES // R:
                        load_residual(n + 1)
                    for m in (2 * n, 2 * n + 1):
                        act.wait_ge(stat_ok, m + 1)
                        act.dma_start(rows(dst, m, 1), res[:, m:m + 1, :]).then_inc(stored, 16)
                act.wait_ge(var_ok, 1)
                nc.scalar.activation(k.std[:, :], k.var[:, :], ACT.Sqrt).then_inc(std_ok, 1)
                act.wait_ge(stored, 16 * TILES)

            @block.tensor
            def _(pe):
                for m in range(TILES):
                    s, t = m // 2 % 2, m % 2
                    pe.wait_ge(ol_ok, m // 2 + 1)
                    if m >= 4:
                        pe.wait_ge(out_ok, m - 3)
                    pairs = [(x[:, g, t * P:(t + 1) * P], w[:, g, :]) for g in range(KC)
                             for x, w in parts_of_product(oh[s], ol[s], k.woh, k.wol)]
                    for i, (x, w) in enumerate(pairs):
                        last = nc.tensor.matmul(py[m % 4][:, :], x, w, start=i == 0, stop=i == len(pairs) - 1)
                    last.then_inc(y_ok, 1)


class Kept:
    pass


def build(nc, d, out):
    k = Kept()
    scratch = lambda n, s: nc.dram_tensor(n, s, F32).ap()
    k.x1 = scratch("x1_scratch", (TOK, C))
    k.x2 = scratch("x2_scratch", (TOK, C))
    k.qh, k.ql, k.kh, k.kl = (scratch(n + "_scratch", (B * C, T)) for n in ("qh", "ql", "kh", "kl"))
    k.v = scratch("v_scratch", (QUADS, T, 4 * ONES))
    k.o = scratch("o_scratch", (QUADS * P, T))
    k.inverse = scratch("inverse_scratch", (QUADS, 4, T))
    k.w2_parts = [scratch(n + "_scratch", (P, HT, C)) for n in ("w2h", "w2l")]
    with ExitStack() as ctx:
        sb = lambda n, s, t: ctx.enter_context(nc.sbuf_tensor(n, s, t))
        k.w1h, k.w1l = sb("w1h", [P, KC, HID], F32R), sb("w1l", [P, KC, HID], F32R)
        k.w3h, k.w3l = sb("w3h", [P, KC, HID], F32R), sb("w3l", [P, KC, HID], F32R)
        k.ident = sb("ident", [P, P], F32)
        k.stats = sb("stats", [P, TILES, 6], F32)
        k.moments = sb("moments", [P, TILES, 2], F32)
        k.mean, k.var = sb("mean", [P, TILES], F32), sb("var", [P, TILES], F32)
        k.std, k.rstd = sb("std", [P, TILES], F32), sb("rstd", [P, TILES], F32)
        k.table_in, k.table_out = sb("table_in", [P, 1], F32), sb("table_out", [P, 1], F32)
        k.rope = sb("rope", [P, 3, QT], F32)
        with ExitStack() as w2:
            k.w2h, k.w2l = [w2.enter_context(nc.sbuf_tensor(n, [P, HT, C], F32R)) for n in ("w2h", "w2l")]
            weights_phase(nc, d, k)
            ffn_phase(nc, k, d["x"], k.x1, "f1_", True)
        with ExitStack() as wo:
            k.woh, k.wol = [wo.enter_context(nc.sbuf_tensor(n, [P, KC, C], F32R)) for n in ("woh", "wol")]
            qkv_phase(nc, d, k, k.x1)
            attention_phase(nc, k)
            project_phase(nc, d, k, k.x1, k.x2)
        with ExitStack() as w2:
            k.w2h, k.w2l = [w2.enter_context(nc.sbuf_tensor(n, [P, HT, C], F32R)) for n in ("w2h_again", "w2l_again")]
            ffn_phase(nc, k, k.x2, out, "f2_", False)


NAMES = {"x": "L0_attn_x", "wq": "L0_attn_wq", "wk": "L0_attn_wk", "wv": "L0_attn_wv", "wo": "L0_attn_wo",
         "w1": "L0_ffn_w1", "s1": "L0_ffn_s1", "w2": "L0_ffn_w2", "s2": "L0_ffn_s2", "w3": "L0_ffn_w3",
         "s3": "L0_ffn_s3"}


def rope_table():
    t = np.arange(T, dtype=np.float32).reshape(QT, P).T
    return np.ascontiguousarray(np.stack([np.cos(t), np.sin(t), -np.sin(t)], axis=1).astype(np.float32))


def kernel(**inputs):
    import numpy as _np
    import concourse.bacc as _bacc
    from concourse import mybir as _mybir
    from concourse.bass_utils import run_bass_kernel_spmd as _run

    nc = _bacc.Bacc("TRN2", target_bir_lowering=False, num_devices=1)
    arrays = {"in_" + n: _np.ascontiguousarray(inputs[full]) for n, full in NAMES.items()}
    arrays["in_x"] = arrays["in_x"].reshape(TOK, C)
    arrays["in_rope"] = rope_table()
    d = {n[3:]: nc.dram_tensor(n, a.shape, _mybir.dt.from_np(a.dtype), kind="ExternalInput").ap()
         for n, a in arrays.items()}
    out = nc.dram_tensor("out", (TOK, C), F32, kind="ExternalOutput").ap()
    build(nc, d, out)
    r = _run(nc, [arrays], core_ids=[0])
    return r.results[0]["out"].reshape(B, T, C)
```
